# Optimizing a Trainium2 kernel written in Bass

```python
import numpy as np
import jax
import jax.numpy as jnp

def _softmax(x, axis=-1):
    return jax.nn.softmax(x, axis=axis)

def _gelu(x):
    return jax.nn.gelu(x, approximate=True)

def _silu(x):
    return jax.nn.silu(x)

def _sigmoid(x):
    return jax.nn.sigmoid(x)

def _layernorm(x, axis=-1, eps=1e-05):
    m = jnp.mean(x, axis=axis, keepdims=True)
    v = jnp.var(x, axis=axis, keepdims=True)
    return (x - m) / jnp.sqrt(v + eps)

def _scatter_add(tgt, idx, src, axis=0):
    return tgt.at[idx].add(src)

def _segment_sum(src, seg, n):
    return jax.ops.segment_sum(src, seg, n)
kernel_name = 'mk_rec_standalone_d1_rec_r8_82b683'

def setup_inputs(seed: int=0):
    np.random.seed(seed)
    _w = jnp.asarray

    def _rec_inputs():
        import jax
        import jax.numpy as jnp
        _rk = jax.random.key(seed)
        r_x_num = -0.00338568 + 1.0005 * jax.random.normal(jax.random.fold_in(_rk, 1), (512, 13), jnp.float32)
        r_x_cat = jnp.stack([jax.random.randint(jax.random.fold_in(jax.random.fold_in(_rk, 2), 0), (512,), 2, 12500, jnp.int32), jax.random.randint(jax.random.fold_in(jax.random.fold_in(_rk, 2), 1), (512,), 1, 99999, jnp.int32), jax.random.randint(jax.random.fold_in(jax.random.fold_in(_rk, 2), 2), (512,), 0, 12500, jnp.int32), jax.random.randint(jax.random.fold_in(jax.random.fold_in(_rk, 2), 3), (512,), 5, 12500, jnp.int32), jax.random.randint(jax.random.fold_in(jax.random.fold_in(_rk, 2), 4), (512,), 20, 99993, jnp.int32), jax.random.randint(jax.random.fold_in(jax.random.fold_in(_rk, 2), 5), (512,), 0, 99993, jnp.int32), jax.random.randint(jax.random.fold_in(jax.random.fold_in(_rk, 2), 6), (512,), 2, 99999, jnp.int32), jax.random.randint(jax.random.fold_in(jax.random.fold_in(_rk, 2), 7), (512,), 2, 99995, jnp.int32), jax.random.randint(jax.random.fold_in(jax.random.fold_in(_rk, 2), 8), (512,), 0, 99999, jnp.int32), jax.random.randint(jax.random.fold_in(jax.random.fold_in(_rk, 2), 9), (512,), 2, 99986, jnp.int32), jax.random.randint(jax.random.fold_in(jax.random.fold_in(_rk, 2), 10), (512,), 4, 99999, jnp.int32), jax.random.randint(jax.random.fold_in(jax.random.fold_in(_rk, 2), 11), (512,), 15, 99999, jnp.int32), jax.random.randint(jax.random.fold_in(jax.random.fold_in(_rk, 2), 12), (512,), 0, 99989, jnp.int32), jax.random.randint(jax.random.fold_in(jax.random.fold_in(_rk, 2), 13), (512,), 5, 99990, jnp.int32), jax.random.randint(jax.random.fold_in(jax.random.fold_in(_rk, 2), 14), (512,), 2, 99996, jnp.int32), jax.random.randint(jax.random.fold_in(jax.random.fold_in(_rk, 2), 15), (512,), 3, 99994, jnp.int32), jax.random.randint(jax.random.fold_in(jax.random.fold_in(_rk, 2), 16), (512,), 0, 99998, jnp.int32), jax.random.randint(jax.random.fold_in(jax.random.fold_in(_rk, 2), 17), (512,), 13, 99998, jnp.int32), jax.random.randint(jax.random.fold_in(jax.random.fold_in(_rk, 2), 18), (512,), 10, 12498, jnp.int32), jax.random.randint(jax.random.fold_in(jax.random.fold_in(_rk, 2), 19), (512,), 0, 99999, jnp.int32), jax.random.randint(jax.random.fold_in(jax.random.fold_in(_rk, 2), 20), (512,), 0, 99995, jnp.int32), jax.random.randint(jax.random.fold_in(jax.random.fold_in(_rk, 2), 21), (512,), 1, 99998, jnp.int32), jax.random.randint(jax.random.fold_in(jax.random.fold_in(_rk, 2), 22), (512,), 1, 99997, jnp.int32), jax.random.randint(jax.random.fold_in(jax.random.fold_in(_rk, 2), 23), (512,), 2, 99989, jnp.int32), jax.random.randint(jax.random.fold_in(jax.random.fold_in(_rk, 2), 24), (512,), 6, 12500, jnp.int32), jax.random.randint(jax.random.fold_in(jax.random.fold_in(_rk, 2), 25), (512,), 2, 99995, jnp.int32)], axis=1)
        return (r_x_num, r_x_cat)
    r_x_num, r_x_cat = _rec_inputs()

    def _L0_rec_setup():
        import jax, jax.numpy as jnp
        import numpy as np
        B = 2048
        N_NUM = 13
        N_FIELDS = 26
        VOCAB = 12500
        K = 64
        HIDDEN = [1024, 512, 256]
        DEEP_IN = N_NUM + N_FIELDS * K
        key = jax.random.key(seed)
        ks = jax.random.split(key, 16)
        x_num = jax.random.normal(ks[0], (B, N_NUM), dtype=jnp.float32)
        x_cat = jax.random.randint(ks[1], (B, N_FIELDS), 0, VOCAB, dtype=jnp.int32)
        bias = jnp.zeros((1,), dtype=jnp.float32)
        w_num = jax.random.normal(ks[2], (N_NUM, 1), dtype=jnp.float32) * 0.1
        lin_cat = jax.random.normal(ks[3], (N_FIELDS, VOCAB, 1), dtype=jnp.float32) * 0.01
        v_num = jax.random.normal(ks[4], (N_NUM, K), dtype=jnp.float32) * 0.01
        v_cat = jax.random.normal(ks[5], (N_FIELDS, VOCAB, K), dtype=jnp.float32) * 0.01
        W1 = jax.random.normal(ks[6], (DEEP_IN, HIDDEN[0]), dtype=jnp.float32) * (1.0 / np.sqrt(DEEP_IN))
        b1 = jnp.zeros((HIDDEN[0],), dtype=jnp.float32)
        W2 = jax.random.normal(ks[7], (HIDDEN[0], HIDDEN[1]), dtype=jnp.float32) * (1.0 / np.sqrt(HIDDEN[0]))
        b2 = jnp.zeros((HIDDEN[1],), dtype=jnp.float32)
        W3 = jax.random.normal(ks[8], (HIDDEN[1], HIDDEN[2]), dtype=jnp.float32) * (1.0 / np.sqrt(HIDDEN[1]))
        b3 = jnp.zeros((HIDDEN[2],), dtype=jnp.float32)
        Wo = jax.random.normal(ks[9], (HIDDEN[2], 1), dtype=jnp.float32) * (1.0 / np.sqrt(HIDDEN[2]))
        bo = jnp.zeros((1,), dtype=jnp.float32)
        return {'x_num': x_num, 'x_cat': x_cat, 'bias': bias, 'w_num': w_num, 'lin_cat': lin_cat, 'v_num': v_num, 'v_cat': v_cat, 'W1': W1, 'b1': b1, 'W2': W2, 'b2': b2, 'W3': W3, 'b3': b3, 'Wo': Wo, 'bo': bo}
    _L0_rec_all = _L0_rec_setup()
    _L0_rec_in = {k: v for k, v in _L0_rec_all.items() if k in ('bias', 'w_num', 'lin_cat', 'v_num', 'v_cat', 'W1', 'b1', 'W2', 'b2', 'W3', 'b3', 'Wo', 'bo')}
    del _L0_rec_all
    return {'r_x_num': r_x_num, 'r_x_cat': r_x_cat, 'L0_rec_bias': _L0_rec_in['bias'], 'L0_rec_w_num': _L0_rec_in['w_num'], 'L0_rec_lin_cat': _L0_rec_in['lin_cat'], 'L0_rec_v_num': _L0_rec_in['v_num'], 'L0_rec_v_cat': _L0_rec_in['v_cat'], 'L0_rec_W1': _L0_rec_in['W1'], 'L0_rec_b1': _L0_rec_in['b1'], 'L0_rec_W2': _L0_rec_in['W2'], 'L0_rec_b2': _L0_rec_in['b2'], 'L0_rec_W3': _L0_rec_in['W3'], 'L0_rec_b3': _L0_rec_in['b3'], 'L0_rec_Wo': _L0_rec_in['Wo'], 'L0_rec_bo': _L0_rec_in['bo']}

def reference(r_x_num, r_x_cat, L0_rec_bias, L0_rec_w_num, L0_rec_lin_cat, L0_rec_v_num, L0_rec_v_cat, L0_rec_W1, L0_rec_b1, L0_rec_W2, L0_rec_b2, L0_rec_W3, L0_rec_b3, L0_rec_Wo, L0_rec_bo):
    import jax
    import jax.numpy as jnp

    def _L0_rec_ref(x_num, x_cat, bias, w_num, lin_cat, v_num, v_cat, W1, b1, W2, b2, W3, b3, Wo, bo):
        import jax, jax.numpy as jnp
        import numpy as np
        B = 2048
        N_NUM = 13
        N_FIELDS = 26
        VOCAB = 12500
        K = 64
        HIDDEN = [1024, 512, 256]
        DEEP_IN = N_NUM + N_FIELDS * K
        fid = jnp.arange(N_FIELDS)[None, :]
        lin = bias + x_num @ w_num + lin_cat[fid, x_cat].sum(axis=1)
        vn = x_num[:, :, None] * v_num[None, :, :]
        vc = v_cat[fid, x_cat]
        v = jnp.concatenate([vn, vc], axis=1)
        sum_v = v.sum(axis=1)
        interactions = 0.5 * (sum_v * sum_v - (v * v).sum(axis=1)).sum(axis=1, keepdims=True)
        deep_in = jnp.concatenate([x_num, vc.reshape(vc.shape[0], -1)], axis=1)
        h = jax.nn.relu(deep_in @ W1 + b1)
        h = jax.nn.relu(h @ W2 + b2)
        h = jax.nn.relu(h @ W3 + b3)
        deep_out = h @ Wo + bo
        return lin + interactions + deep_out
    y = _L0_rec_ref(r_x_num, r_x_cat, L0_rec_bias, L0_rec_w_num, L0_rec_lin_cat, L0_rec_v_num, L0_rec_v_cat, L0_rec_W1, L0_rec_b1, L0_rec_W2, L0_rec_b2, L0_rec_W3, L0_rec_b3, L0_rec_Wo, L0_rec_bo)
    return y

_drawn_inputs = setup_inputs


def setup_inputs(seed=0):
    import zlib

    import numpy as np

    out = dict(_drawn_inputs(seed))
    spreads = {'L0_rec_b1': (0.0, 0.1), 'L0_rec_b2': (0.0, 0.1), 'L0_rec_b3': (0.0, 0.1)}
    factors = {}
    for name, (base, spread) in spreads.items():
        noise = np.random.default_rng([zlib.crc32(name.encode()), seed]).standard_normal(out[name].shape)
        drawn = base * np.exp(spread * noise) if base else spread * noise
        out[name] = jnp.asarray(drawn.astype(out[name].dtype))
    for name, factor in factors.items():
        out[name] = (out[name] * factor).astype(out[name].dtype)
    return out
```

```python
from contextlib import ExitStack

import concourse.bass as bass
from concourse import mybir

P = 128
F32 = mybir.dt.float32
F32R = mybir.dt.float32r
I32 = mybir.dt.int32
ALU = mybir.AluOpType
ACT = mybir.ActivationFunctionType
AX = mybir.AxisListType

NUM = 13
FIELDS, VOCAB, K = 26, 12500, 64
ROW = K + 1
BATCH = 512
TILES = BATCH // P
H1, H2, H3 = 1024, 512, 256
CHUNKS = FIELDS * K // P
GROUPS = (CHUNKS + 1) // 2
HALF = 512
STACK = 32
NV = K + 2

W1_ITEMS, W2_ITEMS, W3_ITEMS = CHUNKS, (H1 // P) * H2 // H1, (H2 // P) * H3 // H1
W_ITEMS = W1_ITEMS + W2_ITEMS + W3_ITEMS
ITEMS = 2 + W_ITEMS
RING = 4


def fields_of(j):
    return 4 * j, min(4 * j + 4, FIELDS)


def chunks_of(j):
    return 2 * j, min(2 * j + 2, CHUNKS)


def x_slot(j):
    return 2 if j == GROUPS - 1 else j % 2


def items_in_group(j):
    cuts = [0, 4, 7, 10, 13, 16, W_ITEMS, W_ITEMS]
    return range(2 + cuts[j], 2 + cuts[j + 1])


def deepfm_kernel(nc, x_cat, table, x_rows, num_weights, num_vectors, biases, row_consts, weights, out):
    with ExitStack() as ctx:
        def sb(name, shape, dt=F32):
            return ctx.enter_context(nc.sbuf_tensor(name, shape, dt))

        def ps(name, shape):
            return ctx.enter_context(nc.psum_tensor(name, shape, F32))

        def sem(name):
            return ctx.enter_context(nc.semaphore(name))

        cat = sb("cat", [P, TILES, FIELDS], I32)
        wrap = sb("wrap", [P, TILES * FIELDS])
        field_base = sb("field_base", [P, TILES, FIELDS], I32)
        row_all = sb("row_all", [P, TILES + 1, FIELDS], I32)
        row_now = sb("row_now", [P, FIELDS], I32)
        g = sb("g", [P, CHUNKS, 2 * ROW])
        ident = sb("ident", [P, P])
        ones = sb("ones", [P, P], F32R)
        raw = sb("raw", [P, RING, H1])
        w_hi = sb("w_hi", [P, W_ITEMS, H1], F32R)
        w_lo = sb("w_lo", [P, W_ITEMS, H1], F32R)
        num_w = sb("num_w", [P, H1], F32R)
        vec_raw = sb("vec_raw", [P, NV])
        num_v = sb("num_v", [P, NV], F32R)
        bias_w = sb("bias_w", [P, HALF], F32R)
        consts = sb("consts", [P, H3 + 2])
        x_num_all = sb("x_num_all", [P, BATCH], F32R)
        x_num_now = sb("x_num_now", [P, P], F32R)
        x_sq = sb("x_sq", [STACK, BATCH])
        v_sq = sb("v_sq", [STACK, 1])
        x_hi = sb("x_hi", [P, 5, P], F32R)
        x_lo = sb("x_lo", [P, 5, P], F32R)
        h1t_hi = sb("h1t_hi", [P, H1 // P, P], F32R)
        h1t_lo = sb("h1t_lo", [P, H1 // P, P], F32R)
        h2t_hi = sb("h2t_hi", [P, H2 // P, P], F32R)
        h2t_lo = sb("h2t_lo", [P, H2 // P, P], F32R)
        junk_sq = sb("junk_sq", [P, 4 * K])
        junk_h3 = sb("junk_h3", [P, H3])
        junk_fm = sb("junk_fm", [P, K])
        field_sum = sb("field_sum", [P, GROUPS, ROW])
        sq_sum = sb("sq_sum", [P, GROUPS])
        num_terms = sb("num_terms", [P, TILES, NV + 2])
        lin_const = sb("lin_const", [P, 1])
        num_sq_half = sb("num_sq_half", [P, TILES])
        s_vec = sb("s_vec", [P, ROW])
        s_all = sb("s_all", [P, ROW])
        fm_a = sb("fm_a", [P, 1])
        fm_b = sb("fm_b", [P, 1])
        fm_c = sb("fm_c", [P, 1])
        fm = sb("fm", [P, 1])
        deep = sb("deep", [P, 1])
        result = sb("result", [P, TILES])
        h1 = raw[:, 0, :]
        h2 = raw[:, 1, 0:H2]

        acc1 = [ps(f"acc1_{i}", [P, HALF]) for i in range(2)]
        xt_ps = [ps(f"xt_ps{i}", [P, HALF]) for i in range(2)]
        ht_ps = [ps(f"ht_ps{i}", [P, HALF]) for i in range(2)]
        acc2 = ps("acc2", [P, HALF])
        acc3 = ps("acc3", [P, HALF])

        cat_in = sem("cat_in")
        small_in = sem("small_in")
        raw_in = [sem(f"raw_in{s}") for s in range(RING)]
        rows_in = [sem(f"rows_in{j}") for j in range(GROUPS)]
        base_made = sem("base_made")
        zeros_made = sem("zeros_made")
        ones_made = sem("ones_made")
        ident_made = sem("ident_made")
        index_step = sem("index_step")
        rows_ready = sem("rows_ready")
        hi_made = sem("hi_made")
        lo_made = sem("lo_made")
        squares_made = sem("squares_made")
        vec_made = sem("vec_made")
        num_ps = sem("num_ps")
        num_step = sem("num_step")
        x_num_ready = sem("x_num_ready")
        num_added = sem("num_added")
        xt_done = sem("xt_done")
        xhi_done = sem("xhi_done")
        xlo_done = sem("xlo_done")
        l1_done = sem("l1_done")
        l1_half0 = sem("l1_half0")
        squared = sem("squared")
        summed = sem("summed")
        relu1a = sem("relu1a")
        relu1b = sem("relu1b")
        h1t_done = sem("h1t_done")
        h1hi_done = sem("h1hi_done")
        h1lo_done = sem("h1lo_done")
        l2_done = sem("l2_done")
        relu2 = sem("relu2")
        h2t_done = sem("h2t_done")
        h2hi_done = sem("h2hi_done")
        h2lo_done = sem("h2lo_done")
        l3_done = sem("l3_done")
        fm_step = sem("fm_step")
        fm_done = sem("fm_done")
        deep_done = sem("deep_done")
        result_done = sem("result_done")
        stored = sem("stored")

        block = ctx.enter_context(nc.Block())

        def x_cols(j):
            c0, c1 = chunks_of(j)
            s = 2 * x_slot(j)
            return slice(s, s + c1 - c0)

        def embeddings(j):
            c0, c1 = chunks_of(j)
            return g[:, c0:c1, 1:1 + 2 * K]

        def linear(j):
            c0, c1 = chunks_of(j)
            return g[:, c0:c1, 0:2 * ROW:2 * ROW - 1]

        @block.sync
        def _(sp):
            sp.dma_start(cat[:, :, :], x_cat.rearrange("(t p) f -> p t f", p=P)).then_inc(cat_in, 16)
            for i in range(ITEMS):
                if i >= RING:
                    sp.wait_ge(hi_made, i - RING + 1)
                    sp.wait_ge(lo_made, i - RING + 1)
                slot = raw[:, i % RING, :]
                if i == 0:
                    sp.dma_start(slot, num_weights).then_inc(raw_in[0], 16)
                elif i == 1:
                    sp.dma_start(slot[:, 0:BATCH], x_rows).then_inc(raw_in[1], 16)
                    sp.dma_start(slot[:, BATCH:BATCH + HALF], biases).then_inc(raw_in[1], 16)
                else:
                    sp.dma_start(slot, weights[i - 2]).then_inc(raw_in[i % RING], 16)
            with sp.Fori(0, TILES) as t:
                sp.wait_ge(result_done, t + 1)
                sp.dma_start(out[bass.ds(t * P, P), :], result[:, bass.ds(t, 1)]).then_inc(stored, 16)
            sp.wait_ge(stored, 16 * TILES)

        @block.gpsimd
        def _(pool):
            pool.iota(field_base[:, :, :], [[0, TILES], [VOCAB, FIELDS]], base=0,
                      channel_multiplier=0).then_inc(base_made, 1)
            pool.memset(row_all[:, TILES, :], 0).then_inc(base_made, 1)
            pool.memset(ident[:, :], 0.0).then_inc(zeros_made, 1)
            pool.wait_ge(zeros_made, 1)
            pool.affine_select(out=ident[:, :], in_=ident[:, :], compare_op=ALU.not_equal, fill=1.0,
                               base=0, pattern=[[-1, P]], channel_multiplier=1).then_inc(ident_made, 1)

            for t in range(TILES):
                for j in range(GROUPS):
                    pool.wait_ge(rows_ready, t * GROUPS + j + 1)
                    if t > 0:
                        pool.wait_ge(xt_done, (t - 1) * GROUPS + j + 1)
                        pool.wait_ge(squared, (t - 1) * GROUPS + j + 1)
                        pool.wait_ge(summed, 2 * ((t - 1) * GROUPS + j + 1))
                    for f in range(*fields_of(j)):
                        pool.indirect_dma_start(
                            g[:, f // 2, (f % 2) * ROW:(f % 2 + 1) * ROW], None, table,
                            bass.IndirectOffsetOnAxis(row_now[:, f:f + 1], 0)).then_inc(rows_in[j], 16)

        def rows_landed(eng, t, j):
            f0, f1 = fields_of(j)
            eng.wait_ge(rows_in[j], (t + 1) * 16 * (f1 - f0))

        def item_landed(eng, i):
            eng.wait_ge(raw_in[i % RING], 16 * (i // RING + 1 + (i % RING == 1)))

        @block.scalar
        def _(act):
            act.dma_start(vec_raw[:, :], num_vectors).then_inc(small_in, 16)
            act.dma_start(consts[:, :], row_consts).then_inc(small_in, 16)

            def high_part(i):
                item_landed(act, i)
                act.activation(w_hi[:, i - 2, :], raw[:, i % RING, :], ACT.Copy).then_inc(hi_made, 1)

            def num_now(t):
                act.activation(x_num_now[:, :], x_num_all[:, bass.ds(t * P, P)].bitcast(F32),
                               ACT.Copy).then_inc(x_num_ready, 1)

            item_landed(act, 0)
            act.activation(num_w[:, :], raw[:, 0, :], ACT.Copy).then_inc(hi_made, 1)
            item_landed(act, 1)
            act.activation(x_sq[:, :], raw[0:STACK, 1, 0:BATCH], ACT.Square).then_inc(squares_made, 1)
            act.wait_ge(small_in, 32)
            act.activation(junk_sq[0:STACK, 0:K], vec_raw[0:STACK, 0:K], ACT.Square,
                           accum_out=v_sq[:, :]).then_inc(squares_made, 1)
            act.activation(num_v[:, :], vec_raw[:, :], ACT.Copy).then_inc(squares_made, 1)
            act.activation(bias_w[:, :], raw[:, 1, BATCH:BATCH + HALF], ACT.Copy)\
               .then_inc(squares_made, 1)
            act.activation(x_num_all[:, :], raw[:, 1, 0:BATCH], ACT.Copy).then_inc(hi_made, 1)
            act.wait_ge(lo_made, 2)
            num_now(0)

            def group(t, j, first):
                n = t * GROUPS + j
                c0, c1 = chunks_of(j)
                width = (c1 - c0) * P
                if 2 <= j < GROUPS - 1:
                    act.wait_ge(l1_done, n - 1)
                elif not first:
                    act.wait_ge(l1_done, {0: n - 2, 1: n - 2, GROUPS - 1: n - GROUPS + 1}[j])
                act.wait_ge(xt_done, n + 1)
                act.activation(x_hi[:, x_cols(j), :], xt_ps[j % 2][:, 0:width], ACT.Copy)\
                   .then_inc(xhi_done, 1)
                f0, f1 = fields_of(j)
                rows_landed(act, t, j)
                if j == 0 and not first:
                    act.wait_ge(fm_done, t)
                if j == 0 and first:
                    act.wait_ge(squares_made, 2)
                else:
                    act.wait_ge(squared, n)
                act.activation(junk_sq[:, 0:(f1 - f0) * K], embeddings(j), ACT.Square,
                               accum_out=sq_sum[:, j:j + 1]).then_inc(squared, 1)

            def hidden1_high(t):
                for a in range(2):
                    act.wait_ge(h1t_done, 2 * t + a + 1)
                    act.activation(h1t_hi[:, 4 * a:4 * a + 4, :], ht_ps[a][:, :], ACT.Copy)\
                       .then_inc(h1hi_done, 1)

            def hidden2_relu(t):
                act.wait_ge(l2_done, t + 1)
                act.activation(h2, acc2[:, :], ACT.Relu).then_inc(relu2, 1)

            def hidden2_high(t):
                act.wait_ge(h2t_done, t + 1)
                act.activation(h2t_hi[:, :, :], ht_ps[0][:, :], ACT.Copy).then_inc(h2hi_done, 1)

            def finish_layer1(t, first):
                if first:
                    act.wait_ge(lo_made, ITEMS)
                act.wait_ge(l1_half0, t + 1)
                act.activation(h1[:, 0:HALF], acc1[0][:, :], ACT.Relu).then_inc(relu1a, 1)

            for j in range(GROUPS):
                for i in items_in_group(j):
                    high_part(i)
                group(0, j, True)
            finish_layer1(0, True)

            def tile(t):
                act.wait_ge(num_added, t)
                num_now(t)
                for j in range(GROUPS):
                    group(t, j, False)
                    if j == 0:
                        hidden1_high(t - 1)
                    if j == 2:
                        hidden2_relu(t - 1)
                    if j == 3:
                        hidden2_high(t - 1)
                finish_layer1(t, False)

            tile(1)
            with act.Fori(2, TILES) as t:
                tile(t)
            hidden1_high(TILES - 1)
            hidden2_relu(TILES - 1)
            hidden2_high(TILES - 1)

        @block.vector
        def _(dve):
            flat = cat[:, :, :].rearrange("p t f -> p (t f)")
            rows = row_all[:, 0:TILES, :].rearrange("p t f -> p (t f)")
            base = field_base[:, :, :].rearrange("p t f -> p (t f)")
            dve.wait_ge(cat_in, 16)
            dve.tensor_scalar(wrap[:, :], flat, 0.0, float(VOCAB), ALU.is_lt, ALU.mult)\
               .then_inc(index_step, 1)
            dve.wait_ge(index_step, 1)
            dve.tensor_tensor(wrap[:, :], wrap[:, :], flat, ALU.add).then_inc(index_step, 1)
            dve.wait_ge(index_step, 2)
            dve.tensor_scalar(wrap[:, :], wrap[:, :], 0.0, float(VOCAB - 1), ALU.max, ALU.min)\
               .then_inc(index_step, 1)
            dve.wait_ge(index_step, 3)
            dve.wait_ge(base_made, 2)
            dve.tensor_tensor(row_now[:, :], wrap[:, 0:FIELDS], base[:, 0:FIELDS], ALU.add)\
               .then_inc(rows_ready, GROUPS)
            dve.tensor_tensor(rows, wrap[:, :], base, ALU.add).then_inc(index_step, 1)
            dve.memset(ones[:, :].bitcast(F32), 1.0).then_inc(ones_made, 1)

            def low_rows(tile, source, lo, hi):
                part = tile[lo:hi, :]
                return dve.tensor_tensor(part, source[lo:hi, :], part.bitcast(F32), ALU.subtract)

            dve.wait_ge(hi_made, 1)
            low_rows(num_w, raw[:, 0, :], STACK, 2 * STACK)
            low_rows(num_w, raw[:, 0, :], 3 * STACK, P).then_inc(lo_made, 1)
            dve.wait_ge(squares_made, 4)
            low_rows(num_v, vec_raw, STACK, 2 * STACK)
            low_rows(num_v, vec_raw, 3 * STACK, P).then_inc(vec_made, 1)
            low_rows(bias_w, raw[:, 1, BATCH:BATCH + HALF], STACK, 2 * STACK)
            low_rows(bias_w, raw[:, 1, BATCH:BATCH + HALF], 3 * STACK, P).then_inc(vec_made, 1)
            dve.wait_ge(hi_made, 2)
            low_rows(x_num_all, raw[:, 1, 0:BATCH], 2 * STACK, P).then_inc(lo_made, 1)

            def low_part(i):
                dve.wait_ge(hi_made, i + 1)
                dve.tensor_tensor(w_lo[:, i - 2, :], raw[:, i % RING, :],
                                  w_hi[:, i - 2, :].bitcast(F32), ALU.subtract).then_inc(lo_made, 1)

            def numeric_terms():
                dve.wait_ge(num_ps, 1)
                terms = acc3[:, 0:TILES * (NV + 2)].rearrange("p (t v) -> p t v", t=TILES)
                dve.tensor_copy(num_terms[:, :, 0:NV + 1], terms[:, :, 0:NV + 1])\
                   .then_inc(num_step, 1)
                dve.wait_ge(small_in, 32)
                dve.tensor_tensor(lin_const[:, :], consts[:, H3:H3 + 1], consts[:, H3 + 1:H3 + 2],
                                  ALU.add).then_inc(num_step, 1)
                dve.wait_ge(num_step, 2)
                dve.tensor_scalar(num_sq_half[:, :], num_terms[:, :, NV], -0.5, lin_const[:, :],
                                  ALU.mult, ALU.add).then_inc(num_step, 1)
                dve.wait_ge(num_step, 3)
                dve.tensor_tensor(num_terms[:, :, K], num_terms[:, :, K], num_sq_half[:, :],
                                  ALU.add).then_inc(num_step, 1)

            def group(t, j):
                n = t * GROUPS + j
                c0, c1 = chunks_of(j)
                width = (c1 - c0) * P
                f0, f1 = fields_of(j)
                dve.wait_ge(xhi_done, n + 1)
                dve.tensor_tensor(x_lo[:, x_cols(j), :],
                                  xt_ps[j % 2][:, 0:width].rearrange("p (c b) -> p c b", b=P),
                                  x_hi[:, x_cols(j), :].bitcast(F32), ALU.subtract).then_inc(xlo_done, 1)
                rows_landed(dve, t, j)
                dve.tensor_reduce(field_sum[:, j, 0:K],
                                  embeddings(j).rearrange("p c (a k) -> p k c a", a=2),
                                  AX.XY, ALU.add).then_inc(summed, 1)
                dve.tensor_reduce(field_sum[:, j, K:ROW], linear(j), AX.XY, ALU.add)\
                   .then_inc(summed, 1)
                dve.tensor_copy(row_now[:, f0:f1], row_all[:, t + 1, f0:f1]).then_inc(rows_ready, 1)

            def hidden1_low(t):
                for a in range(2):
                    dve.wait_ge(h1hi_done, 2 * t + a + 1)
                    dve.tensor_tensor(h1t_lo[:, 4 * a:4 * a + 4, :],
                                      ht_ps[a][:, :].rearrange("p (c b) -> p c b", b=P),
                                      h1t_hi[:, 4 * a:4 * a + 4, :].bitcast(F32), ALU.subtract)\
                       .then_inc(h1lo_done, 1)

            def hidden2_low(t):
                dve.wait_ge(h2hi_done, t + 1)
                dve.tensor_tensor(h2t_lo[:, :, :], ht_ps[0][:, :].rearrange("p (c b) -> p c b", b=P),
                                  h2t_hi[:, :, :].bitcast(F32), ALU.subtract).then_inc(h2lo_done, 1)

            def finish_tile(t):
                dve.wait_ge(l3_done, t + 1)
                dve.scalar_tensor_tensor(junk_h3[:, :], acc3[:, 0:H3], 0.0, consts[:, 0:H3],
                                         ALU.max, ALU.mult, accum_out=deep[:, :]).then_inc(deep_done, 1)
                dve.wait_ge(deep_done, t + 1)
                dve.wait_ge(fm_done, t + 1)
                dve.tensor_tensor(result[:, bass.ds(t, 1)], deep[:, :], fm[:, :], ALU.add).then_inc(result_done, 1)

            def finish_layer1(t, first):
                dve.wait_ge(l1_done, (t + 1) * GROUPS)
                dve.tensor_scalar(h1[:, HALF:H1], acc1[1][:, :], 0.0, None, ALU.max).then_inc(relu1b, 1)
                dve.wait_ge(summed, 2 * (t + 1) * GROUPS)
                dve.tensor_reduce(s_vec[:, :], field_sum[:, :, :].rearrange("p j k -> p k j"), AX.X,
                                  ALU.add).then_inc(fm_step, 1)
                dve.wait_ge(fm_step, 5 * t + 1)
                dve.tensor_tensor(s_all[:, :], s_vec[:, :], num_terms[:, t, 0:ROW], ALU.add)\
                   .then_inc(fm_step, 1)
                dve.wait_ge(squared, (t + 1) * GROUPS)
                dve.tensor_reduce(fm_b[:, :], sq_sum[:, :], AX.X, ALU.add).then_inc(fm_step, 1)
                dve.wait_ge(fm_step, 5 * t + 3)
                dve.tensor_tensor_reduce(junk_fm[:, :], s_all[:, 0:K], s_all[:, 0:K], 0.5, 0.0,
                                         ALU.mult, ALU.add, fm_a[:, :]).then_inc(fm_step, 1)
                dve.scalar_tensor_tensor(fm_c[:, :], fm_b[:, :], -0.5, s_all[:, K:ROW],
                                         ALU.mult, ALU.add).then_inc(fm_step, 1)
                dve.wait_ge(fm_step, 5 * t + 5)
                dve.tensor_tensor(fm[:, :], fm_c[:, :], fm_a[:, :], ALU.add).then_inc(fm_done, 1)

            for j in range(GROUPS):
                for i in items_in_group(j):
                    low_part(i)
                if j == 1:
                    numeric_terms()
                group(0, j)
            dve.wait_ge(num_step, 4)
            finish_layer1(0, True)

            def tile(t):
                for j in range(GROUPS):
                    group(t, j)
                    if j == 0:
                        hidden1_low(t - 1)
                    if j == 3:
                        hidden2_low(t - 1)
                    if j == 4:
                        finish_tile(t - 1)
                finish_layer1(t, False)

            tile(1)
            with dve.Fori(2, TILES) as t:
                tile(t)
            hidden1_low(TILES - 1)
            hidden2_low(TILES - 1)
            finish_tile(TILES - 1)

        @block.tensor
        def _(pe):
            def numeric_terms():
                pe.wait_ge(lo_made, 2)
                pe.wait_ge(vec_made, 2)
                for t in range(TILES):
                    at = t * (NV + 2)
                    pe.matmul(acc3[:, at:at + NV], x_num_all[:, t * P:(t + 1) * P], num_v[:, :],
                              start=True, stop=True)
                    mm = pe.matmul(acc3[:, at + NV:at + NV + 1], x_sq[:, t * P:(t + 1) * P], v_sq[:, :],
                                   start=True, stop=True)
                mm.then_inc(num_ps, 1)

            def turn_rows(t, j, first):
                n = t * GROUPS + j
                if j >= 2:
                    pe.wait_ge(xlo_done, n - 1)
                elif not first:
                    pe.wait_ge(xlo_done, {0: n, 1: n - 2}[j])
                rows_landed(pe, t, j)
                for a, c in enumerate(range(*chunks_of(j))):
                    mm = pe.transpose(xt_ps[j % 2][:, a * P:(a + 1) * P], g[:, c, 1:1 + P],
                                      ident[:, :])
                mm.then_inc(xt_done, 1)

            def start_layer1(t, first):
                pe.wait_ge(x_num_ready, t + 1)
                if not first:
                    pe.wait_ge(relu1a, t)
                    pe.wait_ge(relu1b, t)
                for a in range(2):
                    mm = pe.matmul(acc1[a][:, :], x_num_now[:, :], num_w[:, a * HALF:(a + 1) * HALF],
                                   start=True, stop=False)
                mm.then_inc(num_added, 1)

            def layer1(t, j, first):
                n = t * GROUPS + j
                c0, c1 = chunks_of(j)
                if first:
                    pe.wait_ge(hi_made, 2 + c1)
                    pe.wait_ge(lo_made, 2 + c1)
                pe.wait_ge(xhi_done, n + 1)
                pe.wait_ge(xlo_done, n + 1)
                for c in range(c0, c1):
                    s = 2 * x_slot(j) + c - c0
                    for a in range(2):
                        w = slice(a * HALF, (a + 1) * HALF)
                        pe.matmul(acc1[a][:, :], x_hi[:, s, :], w_hi[:, c, w], start=False, stop=False)
                        pe.matmul(acc1[a][:, :], x_hi[:, s, :], w_lo[:, c, w], start=False, stop=False)
                        mm = pe.matmul(acc1[a][:, :], x_lo[:, s, :], w_hi[:, c, w], start=False,
                                       stop=(c == CHUNKS - 1))
                        if c == CHUNKS - 1 and a == 0:
                            mm.then_inc(l1_half0, 1)
                mm.then_inc(l1_done, 1)

            def turn_hidden1(t, first):
                for a, relu in enumerate((relu1a, relu1b)):
                    pe.wait_ge(relu, t + 1)
                    if a == 0:
                        if not first:
                            pe.wait_ge(h2lo_done, t)
                    elif not first:
                        pe.wait_ge(h1lo_done, 2 * t)
                    for c in range(4):
                        mm = pe.transpose(ht_ps[a][:, c * P:(c + 1) * P],
                                          h1[:, a * HALF + c * P:a * HALF + (c + 1) * P], ident[:, :])
                    mm.then_inc(h1t_done, 1)

            def layer2(t, half, first):
                if half == 0:
                    if not first:
                        pe.wait_ge(relu2, t)
                    pe.matmul(acc2[:, :], ones[0:2 * STACK, :], bias_w[0:2 * STACK, :],
                              start=True, stop=False)
                pe.wait_ge(h1hi_done, 2 * t + half + 1)
                pe.wait_ge(h1lo_done, 2 * t + half + 1)
                for c in range(4 * half, 4 * half + 4):
                    item, at = W1_ITEMS + c // 2, (c % 2) * H2
                    hi, lo = w_hi[:, item, at:at + H2], w_lo[:, item, at:at + H2]
                    pe.matmul(acc2[:, :], h1t_hi[:, c, :], hi, start=False, stop=False)
                    pe.matmul(acc2[:, :], h1t_hi[:, c, :], lo, start=False, stop=False)
                    mm = pe.matmul(acc2[:, :], h1t_lo[:, c, :], hi, start=False, stop=(c == 7))
                if half == 1:
                    mm.then_inc(l2_done, 1)

            def turn_hidden2(t):
                pe.wait_ge(relu2, t + 1)
                pe.wait_ge(h1lo_done, 2 * t + 1)
                for c in range(4):
                    mm = pe.transpose(ht_ps[0][:, c * P:(c + 1) * P], h2[:, c * P:(c + 1) * P],
                                      ident[:, :])
                mm.then_inc(h2t_done, 1)

            def layer3(t, first):
                if first:
                    pe.wait_ge(num_step, 1)
                else:
                    pe.wait_ge(deep_done, t)
                pe.matmul(acc3[:, 0:H3], ones[2 * STACK:P, :], bias_w[2 * STACK:P, 0:H3],
                          start=True, stop=False)
                pe.wait_ge(h2hi_done, t + 1)
                pe.wait_ge(h2lo_done, t + 1)
                for c in range(4):
                    hi = w_hi[:, W1_ITEMS + W2_ITEMS, c * H3:(c + 1) * H3]
                    lo = w_lo[:, W1_ITEMS + W2_ITEMS, c * H3:(c + 1) * H3]
                    pe.matmul(acc3[:, 0:H3], h2t_hi[:, c, :], hi, start=False, stop=False)
                    pe.matmul(acc3[:, 0:H3], h2t_hi[:, c, :], lo, start=False, stop=False)
                    mm = pe.matmul(acc3[:, 0:H3], h2t_lo[:, c, :], hi, start=False, stop=(c == 3))
                mm.then_inc(l3_done, 1)

            pe.wait_ge(ident_made, 1)
            pe.wait_ge(ones_made, 1)
            numeric_terms()
            for j in range(GROUPS):
                turn_rows(0, j, True)
                if j == 0:
                    start_layer1(0, True)
                layer1(0, j, True)
            pe.wait_ge(hi_made, ITEMS)
            pe.wait_ge(lo_made, ITEMS)

            def tile(t, second):
                for j in range(GROUPS):
                    turn_rows(t, j, False)
                    if j == 0:
                        start_layer1(t, False)
                        turn_hidden1(t - 1, second)
                    if j == 1:
                        layer2(t - 1, 0, second)
                    if j == 2:
                        layer2(t - 1, 1, second)
                    if j == 3:
                        turn_hidden2(t - 1)
                    if j == 4:
                        layer3(t - 1, second)
                    layer1(t, j, False)

            tile(1, True)
            with pe.Fori(2, TILES) as t:
                tile(t, False)
            turn_hidden1(TILES - 1, False)
            layer2(TILES - 1, 0, False)
            layer2(TILES - 1, 1, False)
            turn_hidden2(TILES - 1)
            layer3(TILES - 1, False)


def kernel(r_x_num, r_x_cat, L0_rec_bias, L0_rec_w_num, L0_rec_lin_cat, L0_rec_v_num, L0_rec_v_cat,
           L0_rec_W1, L0_rec_b1, L0_rec_W2, L0_rec_b2, L0_rec_W3, L0_rec_b3, L0_rec_Wo, L0_rec_bo):
    import numpy as np
    import concourse.bacc as bacc
    from concourse.bass_utils import run_bass_kernel_spmd

    f32 = np.float32
    x_num, x_cat = np.asarray(r_x_num), np.ascontiguousarray(r_x_cat)
    W1, W2, W3 = np.asarray(L0_rec_W1), np.asarray(L0_rec_W2), np.asarray(L0_rec_W3)
    v_cat, lin_cat = np.asarray(L0_rec_v_cat), np.asarray(L0_rec_lin_cat)
    table = np.empty((FIELDS, VOCAB, ROW), f32)
    table[0::2, :, 1:], table[0::2, :, :1] = v_cat[0::2], lin_cat[0::2]
    table[1::2, :, :K], table[1::2, :, K:] = v_cat[1::2], lin_cat[1::2]
    table = table.reshape(FIELDS * VOCAB, ROW)
    x_rows = np.zeros((4, STACK, BATCH), f32)
    x_rows[:, :NUM] = x_num.T
    x_rows[:, NUM] = 1.0
    num_weights = np.zeros((4, STACK, H1), f32)
    num_weights[:, :NUM] = W1[:NUM]
    num_weights[:, NUM] = np.asarray(L0_rec_b1)
    num_vectors = np.zeros((4, STACK, NV), f32)
    num_vectors[:, :NUM, :K] = np.asarray(L0_rec_v_num)
    num_vectors[:, :NUM, K:K + 1] = np.asarray(L0_rec_w_num)
    biases = np.zeros((4, STACK, HALF), f32)
    biases[0:2, 0, :H2] = np.asarray(L0_rec_b2)
    biases[2:4, 0, :H3] = np.asarray(L0_rec_b3)
    row_consts = np.empty((P, H3 + 2), f32)
    row_consts[:, :H3] = np.asarray(L0_rec_Wo)[:, 0]
    row_consts[:, H3] = np.asarray(L0_rec_bias)
    row_consts[:, H3 + 1] = np.asarray(L0_rec_bo)
    weights = np.concatenate([
        W1[NUM:].reshape(W1_ITEMS, P, H1),
        W2.reshape(W2_ITEMS, 2, P, H2).transpose(0, 2, 1, 3).reshape(W2_ITEMS, P, H1),
        W3.reshape(W3_ITEMS, 4, P, H3).transpose(0, 2, 1, 3).reshape(W3_ITEMS, P, H1)])
    arrays = {"x_cat": x_cat, "table": table, "x_rows": x_rows.reshape(P, BATCH),
              "num_weights": num_weights.reshape(P, H1), "num_vectors": num_vectors.reshape(P, NV),
              "biases": biases.reshape(P, HALF), "row_consts": row_consts, "weights": weights}
    nc = bacc.Bacc("TRN2", target_bir_lowering=False, num_devices=1)
    args = [nc.dram_tensor(f"in_{name}", a.shape, mybir.dt.from_np(a.dtype), kind="ExternalInput").ap()
            for name, a in arrays.items()]
    out = nc.dram_tensor("out", (BATCH, 1), F32, kind="ExternalOutput").ap()
    deepfm_kernel(nc, *args, out)
    r = run_bass_kernel_spmd(nc, [{f"in_{name}": a for name, a in arrays.items()}], core_ids=[0])
    return r.results[0]["out"]
```

```python
from contextlib import ExitStack

import concourse.bass as bass
from concourse import mybir

P = 128
F32 = mybir.dt.float32
F32R = mybir.dt.float32r
BF16 = mybir.dt.bfloat16
I32 = mybir.dt.int32
ALU = mybir.AluOpType
ACT = mybir.ActivationFunctionType
AX = mybir.AxisListType

NUM = 13
FIELDS, VOCAB, K = 26, 12500, 64
ROW = K + 1
BATCH = 512
TILES = BATCH // P
H1, H2, H3 = 1024, 512, 256
CHUNKS = FIELDS * K // P
GROUPS = (CHUNKS + 1) // 2
HALF = 512
STACK = 32
NV = K + 2

W1_ITEMS, W2_ITEMS, W3_ITEMS = CHUNKS, (H1 // P) * H2 // H1, (H2 // P) * H3 // H1
W_ITEMS = W1_ITEMS + W2_ITEMS + W3_ITEMS
ITEMS = 2 + W_ITEMS
RING = 4


def fields_of(j):
    return 4 * j, min(4 * j + 4, FIELDS)


def chunks_of(j):
    return 2 * j, min(2 * j + 2, CHUNKS)


def x_slot(j):
    return 2 if j == GROUPS - 1 else j % 2


def items_in_group(j):
    return range(2 + chunks_of(j)[0], 2 + chunks_of(j)[1])


LATER_ITEMS = range(2 + W1_ITEMS, ITEMS - 3), range(ITEMS - 3, ITEMS)


def deepfm_kernel(nc, x_cat, table, x_rows, num_weights, num_vectors, row_consts, weights, out):
    with ExitStack() as ctx:
        def sb(name, shape, dt=F32):
            return ctx.enter_context(nc.sbuf_tensor(name, shape, dt))

        def ps(name, shape):
            return ctx.enter_context(nc.psum_tensor(name, shape, F32))

        def sem(name):
            return ctx.enter_context(nc.semaphore(name))

        cat = sb("cat", [P, TILES, FIELDS], I32)
        wrap = sb("wrap", [P, TILES * FIELDS])
        field_base = sb("field_base", [P, TILES, FIELDS], I32)
        row_all = sb("row_all", [P, TILES + 1, FIELDS], I32)
        row_now = sb("row_now", [P, FIELDS], I32)
        g = sb("g", [P, CHUNKS, 2 * ROW])
        ident = sb("ident", [P, P])
        ones = sb("ones", [P, P], F32R)
        raw = sb("raw", [P, RING, H1])
        w_hi = sb("w_hi", [P, W_ITEMS, H1], F32R)
        w_lo = sb("w_lo", [P, W_ITEMS, H1], F32R)
        num_w = sb("num_w", [P, H1], F32R)
        num_v = sb("num_v", [P, NV], F32R)
        bias_w = sb("bias_w", [P, HALF], F32R)
        consts = sb("consts", [P, H3 + 2])
        x_num_all = sb("x_num_all", [P, BATCH], F32R)
        x_num_now = sb("x_num_now", [P, P], F32R)
        v_sq = sb("v_sq", [STACK, 1])
        x_hi = sb("x_hi", [P, 5, P], F32R)
        x_lo = sb("x_lo", [P, 5, P], F32R)
        h1t_hi = sb("h1t_hi", [P, H1 // P, P], F32R)
        h1t_lo = sb("h1t_lo", [P, H1 // P, P], F32R)
        h2t_hi = sb("h2t_hi", [P, H2 // P, P], F32R)
        h2t_lo = sb("h2t_lo", [P, H2 // P, P], F32R)
        junk_sq = sb("junk_sq", [P, 4 * K], BF16)
        junk_h3 = sb("junk_h3", [P, H3], BF16)
        junk_fm = sb("junk_fm", [P, K], BF16)
        field_sum = sb("field_sum", [P, GROUPS, ROW])
        sq_sum = sb("sq_sum", [P, GROUPS])
        num_terms = sb("num_terms", [P, TILES, NV + 2])
        lin_const = sb("lin_const", [P, 1])
        num_sq_half = sb("num_sq_half", [P, TILES])
        s_vec = sb("s_vec", [P, ROW])
        s_all = sb("s_all", [P, ROW])
        fm_a = sb("fm_a", [P, 1])
        fm_b = sb("fm_b", [P, 1])
        fm_c = sb("fm_c", [P, 1])
        fm = sb("fm", [P, TILES])
        deep = sb("deep", [P, 1])
        result = sb("result", [P, TILES])
        h1 = sb("h1", [P, H1])
        h2 = sb("h2", [P, H2])
        x_sq = h1[0:STACK, 0:BATCH]
        vec_raw = h1[0:STACK, BATCH:BATCH + NV + H3]

        acc1 = [ps(f"acc1_{i}", [P, HALF]) for i in range(2)]
        xt_ps = [ps(f"xt_ps{i}", [P, HALF]) for i in range(2)]
        ht_ps = [ps(f"ht_ps{i}", [P, HALF]) for i in range(2)]
        acc2 = ps("acc2", [P, HALF])
        acc3 = ps("acc3", [P, HALF])

        cat_in = sem("cat_in")
        small_in = sem("small_in")
        raw_in = [sem(f"raw_in{s}") for s in range(RING)]
        rows_in = [sem(f"rows_in{j}") for j in range(GROUPS)]
        base_made = sem("base_made")
        zeros_made = sem("zeros_made")
        ones_made = sem("ones_made")
        ident_made = sem("ident_made")
        index_step = sem("index_step")
        rows_ready = sem("rows_ready")
        hi_made = sem("hi_made")
        lo_made = sem("lo_made")
        squares_made = sem("squares_made")
        num_lo_made = sem("num_lo_made")
        num_ps = sem("num_ps")
        num_step = sem("num_step")
        x_num_ready = sem("x_num_ready")
        num_added = sem("num_added")
        xt_done = sem("xt_done")
        xhi_done = sem("xhi_done")
        xlo_done = sem("xlo_done")
        l1_done = sem("l1_done")
        l1_half0 = sem("l1_half0")
        squared = sem("squared")
        summed = sem("summed")
        relu1a = sem("relu1a")
        relu1b = sem("relu1b")
        h1t_done = sem("h1t_done")
        h1hi_done = sem("h1hi_done")
        h1lo_done = sem("h1lo_done")
        l2_done = sem("l2_done")
        relu2 = sem("relu2")
        h2t_done = sem("h2t_done")
        h2hi_done = sem("h2hi_done")
        h2lo_done = sem("h2lo_done")
        l3_done = sem("l3_done")
        fm_step = sem("fm_step")
        fm_done = sem("fm_done")
        acc3_read = sem("acc3_read")
        result_done = sem("result_done")
        stored = sem("stored")

        block = ctx.enter_context(nc.Block())

        def x_cols(j):
            c0, c1 = chunks_of(j)
            s = 2 * x_slot(j)
            return slice(s, s + c1 - c0)

        def embeddings(j):
            c0, c1 = chunks_of(j)
            return g[:, c0:c1, 1:1 + 2 * K]

        def linear(j):
            c0, c1 = chunks_of(j)
            return g[:, c0:c1, 0:2 * ROW:2 * ROW - 1]

        @block.sync
        def _(sp):
            sp.dma_start(cat[:, :, :], x_cat.rearrange("(t p) f -> p t f", p=P)).then_inc(cat_in, 16)
            for i in range(ITEMS):
                if i >= RING:
                    sp.wait_ge(hi_made, i - RING + 1)
                    sp.wait_ge(lo_made, i - RING + 1)
                slot = raw[:, i % RING, :]
                if i == 0:
                    sp.dma_start(slot[0:STACK, :], num_weights).then_inc(raw_in[0], 16)
                elif i == 1:
                    sp.dma_start(slot[0:STACK, :], x_rows).then_inc(raw_in[1], 16)
                else:
                    sp.dma_start(slot, weights[i - 2]).then_inc(raw_in[i % RING], 16)
            with sp.Fori(0, TILES) as t:
                sp.wait_ge(result_done, t + 1)
                sp.dma_start(out[bass.ds(t * P, P), :], result[:, bass.ds(t, 1)]).then_inc(stored, 16)
            sp.wait_ge(stored, 16 * TILES)

        @block.gpsimd
        def _(pool):
            pool.iota(field_base[:, :, :], [[0, TILES], [VOCAB, FIELDS]], base=0,
                      channel_multiplier=0).then_inc(base_made, 1)
            pool.memset(row_all[:, TILES, :], 0).then_inc(base_made, 1)
            pool.memset(ident[:, :], 0.0).then_inc(zeros_made, 1)
            pool.wait_ge(zeros_made, 1)
            pool.affine_select(out=ident[:, :], in_=ident[:, :], compare_op=ALU.not_equal, fill=1.0,
                               base=0, pattern=[[-1, P]], channel_multiplier=1).then_inc(ident_made, 1)

            for t in range(TILES):
                for j in range(GROUPS):
                    pool.wait_ge(rows_ready, t * GROUPS + j + 1)
                    if t > 0:
                        pool.wait_ge(xt_done, (t - 1) * GROUPS + j + 1)
                        pool.wait_ge(squared, (t - 1) * GROUPS + j + 1)
                        pool.wait_ge(summed, 2 * ((t - 1) * GROUPS + j + 1))
                    for f in range(*fields_of(j)):
                        pool.indirect_dma_start(
                            g[:, f // 2, (f % 2) * ROW:(f % 2 + 1) * ROW], None, table,
                            bass.IndirectOffsetOnAxis(row_now[:, f:f + 1], 0)).then_inc(rows_in[j], 16)

        def rows_landed(eng, t, j):
            f0, f1 = fields_of(j)
            eng.wait_ge(rows_in[j], (t + 1) * 16 * (f1 - f0))

        def item_landed(eng, i):
            eng.wait_ge(raw_in[i % RING], 16 * (i // RING + 1))

        @block.scalar
        def _(act):
            act.dma_start(vec_raw, num_vectors).then_inc(small_in, 16)
            act.dma_start(consts[:, :], row_consts).then_inc(small_in, 16)

            def high_part(i):
                item_landed(act, i)
                act.activation(w_hi[:, i - 2, :], raw[:, i % RING, :], ACT.Copy).then_inc(hi_made, 1)

            def num_now(t):
                act.activation(x_num_now[:, :], x_num_all[:, bass.ds(t * P, P)].bitcast(F32),
                               ACT.Copy).then_inc(x_num_ready, 1)

            def high_stacks(tile, source, *stacks):
                for k in stacks:
                    last = act.activation(tile[k * STACK:(k + 1) * STACK, 0:source.shape[1]], source,
                                          ACT.Copy)
                return last

            item_landed(act, 0)
            high_stacks(num_w, raw[0:STACK, 0, :], 0, 2).then_inc(hi_made, 1)
            item_landed(act, 1)
            high_stacks(x_num_all, raw[0:STACK, 1, 0:BATCH], 0, 1).then_inc(hi_made, 1)
            act.activation(x_sq, raw[0:STACK, 1, 0:BATCH], ACT.Square).then_inc(squares_made, 1)
            high_stacks(bias_w, raw[0:STACK, 1, BATCH:BATCH + H2], 0).then_inc(squares_made, 1)
            act.wait_ge(small_in, 32)
            high_stacks(bias_w, vec_raw[:, NV:NV + H3], 2).then_inc(squares_made, 1)
            high_stacks(num_v, vec_raw[:, 0:NV], 0, 2).then_inc(squares_made, 1)
            act.activation(junk_sq[0:STACK, 0:K], vec_raw[:, 0:K], ACT.Square,
                           accum_out=v_sq[:, :]).then_inc(squares_made, 1)
            act.wait_ge(num_lo_made, 1)
            num_now(0)

            def group(t, j, first):
                n = t * GROUPS + j
                c0, c1 = chunks_of(j)
                width = (c1 - c0) * P
                if 2 <= j < GROUPS - 1:
                    act.wait_ge(l1_done, n - 1)
                elif not first:
                    act.wait_ge(l1_done, {0: n - 2, 1: n - 2, GROUPS - 1: n - GROUPS + 1}[j])
                act.wait_ge(xt_done, n + 1)
                act.activation(x_hi[:, x_cols(j), :], xt_ps[j % 2][:, 0:width], ACT.Copy)\
                   .then_inc(xhi_done, 1)
                f0, f1 = fields_of(j)
                rows_landed(act, t, j)
                if j == 0 and not first:
                    act.wait_ge(fm_done, t)
                if j == 0 and first:
                    act.wait_ge(squares_made, 5)
                else:
                    act.wait_ge(squared, n)
                act.activation(junk_sq[:, 0:(f1 - f0) * K], embeddings(j), ACT.Square,
                               accum_out=sq_sum[:, j:j + 1]).then_inc(squared, 1)

            def hidden1_high(t):
                for a in range(2):
                    act.wait_ge(h1t_done, 2 * t + a + 1)
                    act.activation(h1t_hi[:, 4 * a:4 * a + 4, :], ht_ps[a][:, :], ACT.Copy)\
                       .then_inc(h1hi_done, 1)

            def hidden2_relu(t):
                act.wait_ge(l2_done, t + 1)
                act.activation(h2[:, :], acc2[:, :], ACT.Relu).then_inc(relu2, 1)

            def hidden2_high(t):
                act.wait_ge(h2t_done, t + 1)
                act.activation(h2t_hi[:, :, :], ht_ps[0][:, :], ACT.Copy).then_inc(h2hi_done, 1)

            def hidden1_relu(t):
                act.wait_ge(l1_half0, t + 1)
                act.activation(h1[:, 0:HALF], acc1[0][:, :], ACT.Relu).then_inc(relu1a, 1)

            def tile(t, second):
                act.wait_ge(num_added, t)
                num_now(t)
                hidden1_relu(t - 1)
                if second:
                    for i in LATER_ITEMS[0]:
                        high_part(i)
                hidden1_high(t - 1)
                group(t, 0, False)
                if second:
                    for i in LATER_ITEMS[1]:
                        high_part(i)
                group(t, 1, False)
                group(t, 2, False)
                hidden2_relu(t - 1)
                group(t, 3, False)
                hidden2_high(t - 1)
                for j in range(4, GROUPS):
                    group(t, j, False)

            for j in range(GROUPS):
                for i in items_in_group(j):
                    high_part(i)
                group(0, j, True)
            tile(1, True)
            with act.Fori(2, TILES) as t:
                tile(t, False)
            hidden1_relu(TILES - 1)
            hidden1_high(TILES - 1)
            hidden2_relu(TILES - 1)
            hidden2_high(TILES - 1)

        @block.vector
        def _(dve):
            flat = cat[:, :, :].rearrange("p t f -> p (t f)")
            rows = row_all[:, 0:TILES, :].rearrange("p t f -> p (t f)")
            base = field_base[:, :, :].rearrange("p t f -> p (t f)")
            dve.wait_ge(cat_in, 16)
            dve.tensor_scalar(wrap[:, :], flat, 0.0, float(VOCAB), ALU.is_lt, ALU.mult)\
               .then_inc(index_step, 1)
            dve.wait_ge(index_step, 1)
            dve.tensor_tensor(wrap[:, :], wrap[:, :], flat, ALU.add).then_inc(index_step, 1)
            dve.wait_ge(index_step, 2)
            dve.tensor_scalar(wrap[:, :], wrap[:, :], 0.0, float(VOCAB - 1), ALU.max, ALU.min)\
               .then_inc(index_step, 1)
            dve.wait_ge(index_step, 3)
            dve.wait_ge(base_made, 2)
            dve.tensor_tensor(row_now[:, :], wrap[:, 0:FIELDS], base[:, 0:FIELDS], ALU.add)\
               .then_inc(rows_ready, GROUPS)
            dve.tensor_tensor(rows, wrap[:, :], base, ALU.add).then_inc(index_step, 1)
            dve.memset(ones[:, :].bitcast(F32), 1.0).then_inc(ones_made, 1)

            def low_stacks(tile, source, high, *stacks):
                cols = slice(0, source.shape[1])
                for k in stacks:
                    last = dve.tensor_tensor(tile[k * STACK:(k + 1) * STACK, cols], source,
                                             tile[high * STACK:(high + 1) * STACK, cols].bitcast(F32),
                                             ALU.subtract)
                return last

            dve.wait_ge(hi_made, 1)
            low_stacks(num_w, raw[0:STACK, 0, :], 0, 1, 3).then_inc(lo_made, 1)
            dve.wait_ge(hi_made, 2)
            low_stacks(x_num_all, raw[0:STACK, 1, 0:BATCH], 0, 2, 3).then_inc(num_lo_made, 1)
            dve.wait_ge(squares_made, 5)
            low_stacks(bias_w, raw[0:STACK, 1, BATCH:BATCH + H2], 0, 1).then_inc(lo_made, 1)
            low_stacks(bias_w, vec_raw[:, NV:NV + H3], 2, 3).then_inc(num_lo_made, 1)
            low_stacks(num_v, vec_raw[:, 0:NV], 0, 1, 3).then_inc(num_lo_made, 1)

            def low_part(i):
                dve.wait_ge(hi_made, i + 1)
                dve.tensor_tensor(w_lo[:, i - 2, :], raw[:, i % RING, :],
                                  w_hi[:, i - 2, :].bitcast(F32), ALU.subtract).then_inc(lo_made, 1)

            def numeric_terms():
                dve.wait_ge(num_ps, 1)
                terms = acc3[:, 0:TILES * (NV + 2)].rearrange("p (t v) -> p t v", t=TILES)
                dve.tensor_copy(num_terms[:, :, 0:NV + 1], terms[:, :, 0:NV + 1])\
                   .then_inc(acc3_read, 1)
                dve.wait_ge(small_in, 32)
                dve.tensor_tensor(lin_const[:, :], consts[:, H3:H3 + 1], consts[:, H3 + 1:H3 + 2],
                                  ALU.add).then_inc(num_step, 1)
                dve.wait_ge(acc3_read, 1)
                dve.wait_ge(num_step, 1)
                dve.tensor_scalar(num_sq_half[:, :], num_terms[:, :, NV], -0.5, lin_const[:, :],
                                  ALU.mult, ALU.add).then_inc(num_step, 1)
                dve.wait_ge(num_step, 2)
                dve.tensor_tensor(num_terms[:, :, K], num_terms[:, :, K], num_sq_half[:, :],
                                  ALU.add).then_inc(num_step, 1)

            def group(t, j):
                n = t * GROUPS + j
                c0, c1 = chunks_of(j)
                width = (c1 - c0) * P
                f0, f1 = fields_of(j)
                dve.wait_ge(xhi_done, n + 1)
                dve.tensor_tensor(x_lo[:, x_cols(j), :],
                                  xt_ps[j % 2][:, 0:width].rearrange("p (c b) -> p c b", b=P),
                                  x_hi[:, x_cols(j), :].bitcast(F32), ALU.subtract).then_inc(xlo_done, 1)
                rows_landed(dve, t, j)
                dve.tensor_reduce(field_sum[:, j, 0:K],
                                  embeddings(j).rearrange("p c (a k) -> p k c a", a=2),
                                  AX.XY, ALU.add).then_inc(summed, 1)
                dve.tensor_reduce(field_sum[:, j, K:ROW], linear(j), AX.XY, ALU.add)\
                   .then_inc(summed, 1)
                dve.tensor_copy(row_now[:, f0:f1], row_all[:, t + 1, f0:f1]).then_inc(rows_ready, 1)

            def hidden1_low(t):
                for a in range(2):
                    dve.wait_ge(h1hi_done, 2 * t + a + 1)
                    dve.tensor_tensor(h1t_lo[:, 4 * a:4 * a + 4, :],
                                      ht_ps[a][:, :].rearrange("p (c b) -> p c b", b=P),
                                      h1t_hi[:, 4 * a:4 * a + 4, :].bitcast(F32), ALU.subtract)\
                       .then_inc(h1lo_done, 1)

            def hidden2_low(t):
                dve.wait_ge(h2hi_done, t + 1)
                dve.tensor_tensor(h2t_lo[:, :, :], ht_ps[0][:, :].rearrange("p (c b) -> p c b", b=P),
                                  h2t_hi[:, :, :].bitcast(F32), ALU.subtract).then_inc(h2lo_done, 1)

            def finish_tile(t):
                dve.wait_ge(l3_done, t + 1)
                dve.scalar_tensor_tensor(junk_h3[:, :], acc3[:, 0:H3], 0.0, consts[:, 0:H3],
                                         ALU.max, ALU.mult, accum_out=deep[:, :]).then_inc(acc3_read, 1)
                dve.wait_ge(acc3_read, t + 2)
                dve.wait_ge(fm_done, t + 1)
                dve.tensor_tensor(result[:, bass.ds(t, 1)], deep[:, :], fm[:, bass.ds(t, 1)], ALU.add).then_inc(result_done, 1)

            def hidden1_relu(t):
                dve.wait_ge(l1_done, (t + 1) * GROUPS)
                dve.tensor_scalar(h1[:, HALF:H1], acc1[1][:, :], 0.0, None, ALU.max).then_inc(relu1b, 1)

            def interactions(t):
                dve.wait_ge(summed, 2 * (t + 1) * GROUPS)
                dve.tensor_reduce(s_vec[:, :], field_sum[:, :, :].rearrange("p j k -> p k j"), AX.X,
                                  ALU.add).then_inc(fm_step, 1)
                dve.wait_ge(fm_step, 5 * t + 1)
                dve.tensor_tensor(s_all[:, :], s_vec[:, :], num_terms[:, t, 0:ROW], ALU.add)\
                   .then_inc(fm_step, 1)
                dve.wait_ge(squared, (t + 1) * GROUPS)
                dve.tensor_reduce(fm_b[:, :], sq_sum[:, :], AX.X, ALU.add).then_inc(fm_step, 1)
                dve.wait_ge(fm_step, 5 * t + 3)
                dve.tensor_tensor_reduce(junk_fm[:, :], s_all[:, 0:K], s_all[:, 0:K], 0.5, 0.0,
                                         ALU.mult, ALU.add, fm_a[:, :]).then_inc(fm_step, 1)
                dve.scalar_tensor_tensor(fm_c[:, :], fm_b[:, :], -0.5, s_all[:, K:ROW],
                                         ALU.mult, ALU.add).then_inc(fm_step, 1)
                dve.wait_ge(fm_step, 5 * t + 5)
                dve.tensor_tensor(fm[:, bass.ds(t, 1)], fm_c[:, :], fm_a[:, :], ALU.add).then_inc(fm_done, 1)

            def tile(t, second):
                hidden1_relu(t - 1)
                if second:
                    for i in LATER_ITEMS[0]:
                        low_part(i)
                else:
                    finish_tile(t - 2)
                hidden1_low(t - 1)
                group(t, 0)
                if second:
                    for i in LATER_ITEMS[1]:
                        low_part(i)
                for j in range(1, 4):
                    group(t, j)
                hidden2_low(t - 1)
                for j in range(4, GROUPS):
                    group(t, j)
                interactions(t)

            for j in range(GROUPS):
                for i in items_in_group(j):
                    low_part(i)
                group(0, j)
                if j == 0:
                    numeric_terms()
            dve.wait_ge(num_step, 3)
            interactions(0)
            tile(1, True)
            with dve.Fori(2, TILES) as t:
                tile(t, False)
            hidden1_relu(TILES - 1)
            finish_tile(TILES - 2)
            hidden1_low(TILES - 1)
            hidden2_low(TILES - 1)
            finish_tile(TILES - 1)

        @block.tensor
        def _(pe):
            def numeric_terms():
                pe.wait_ge(lo_made, 2)
                pe.wait_ge(num_lo_made, 3)
                for t in range(TILES):
                    at = t * (NV + 2)
                    pe.matmul(acc3[:, at:at + NV], x_num_all[:, t * P:(t + 1) * P], num_v[:, :],
                              start=True, stop=True)
                    mm = pe.matmul(acc3[:, at + NV:at + NV + 1], x_sq[:, t * P:(t + 1) * P], v_sq[:, :],
                                   start=True, stop=True)
                mm.then_inc(num_ps, 1)

            def turn_rows(t, j, first):
                n = t * GROUPS + j
                if j >= 2:
                    pe.wait_ge(xlo_done, n - 1)
                elif not first:
                    pe.wait_ge(xlo_done, {0: n, 1: n - 2}[j])
                rows_landed(pe, t, j)
                for a, c in enumerate(range(*chunks_of(j))):
                    mm = pe.transpose(xt_ps[j % 2][:, a * P:(a + 1) * P], g[:, c, 1:1 + P],
                                      ident[:, :])
                mm.then_inc(xt_done, 1)

            def start_layer1(t, first):
                pe.wait_ge(x_num_ready, t + 1)
                if not first:
                    pe.wait_ge(relu1a, t)
                    pe.wait_ge(relu1b, t)
                for a in range(2):
                    mm = pe.matmul(acc1[a][:, :], x_num_now[:, :], num_w[:, a * HALF:(a + 1) * HALF],
                                   start=True, stop=False)
                mm.then_inc(num_added, 1)

            def layer1(t, c, first):
                j = c // 2
                n = t * GROUPS + j
                last = c == CHUNKS - 1
                at = 2 * x_slot(j) + c % 2
                halves = [(acc1[a][:, :], slice(a * HALF, (a + 1) * HALF)) for a in range(2)]
                if first:
                    pe.wait_ge(hi_made, 2 + c + 1)
                    pe.wait_ge(lo_made, 2 + c + 1)
                pe.wait_ge(xhi_done, n + 1)
                for acc, w in halves:
                    pe.matmul(acc, x_hi[:, at, :], w_hi[:, c, w], start=False, stop=False)
                    pe.matmul(acc, x_hi[:, at, :], w_lo[:, c, w], start=False, stop=False)
                pe.wait_ge(xlo_done, n + 1)
                for a, (acc, w) in enumerate(halves):
                    mm = pe.matmul(acc, x_lo[:, at, :], w_hi[:, c, w], start=False, stop=last)
                    if last and a == 0:
                        mm.then_inc(l1_half0, 1)
                if last or c % 2:
                    mm.then_inc(l1_done, 1)

            def turn_hidden1(t, first):
                for a, relu in enumerate((relu1a, relu1b)):
                    pe.wait_ge(relu, t + 1)
                    if a == 0:
                        if not first:
                            pe.wait_ge(h2lo_done, t)
                    elif not first:
                        pe.wait_ge(h1lo_done, 2 * t)
                    for c in range(4):
                        mm = pe.transpose(ht_ps[a][:, c * P:(c + 1) * P],
                                          h1[:, a * HALF + c * P:a * HALF + (c + 1) * P], ident[:, :])
                    mm.then_inc(h1t_done, 1)

            def layer2(t, half, first):
                if half == 0:
                    if not first:
                        pe.wait_ge(relu2, t)
                    pe.matmul(acc2[:, :], ones[0:2 * STACK, :], bias_w[0:2 * STACK, :],
                              start=True, stop=False)
                chunks = [(c, W1_ITEMS + c // 2, slice(c % 2 * H2, (c % 2 + 1) * H2))
                          for c in range(4 * half, 4 * half + 4)]
                if first:
                    split = 2 + W1_ITEMS + 2 * half + 2
                    pe.wait_ge(hi_made, split)
                    pe.wait_ge(lo_made, split)
                pe.wait_ge(h1hi_done, 2 * t + half + 1)
                for c, i, w in chunks:
                    pe.matmul(acc2[:, :], h1t_hi[:, c, :], w_hi[:, i, w], start=False, stop=False)
                    pe.matmul(acc2[:, :], h1t_hi[:, c, :], w_lo[:, i, w], start=False, stop=False)
                pe.wait_ge(h1lo_done, 2 * t + half + 1)
                for c, i, w in chunks:
                    mm = pe.matmul(acc2[:, :], h1t_lo[:, c, :], w_hi[:, i, w], start=False,
                                   stop=(c == H1 // P - 1))
                if half == 1:
                    mm.then_inc(l2_done, 1)

            def turn_hidden2(t):
                pe.wait_ge(relu2, t + 1)
                pe.wait_ge(h1lo_done, 2 * t + 1)
                for c in range(4):
                    mm = pe.transpose(ht_ps[0][:, c * P:(c + 1) * P], h2[:, c * P:(c + 1) * P],
                                      ident[:, :])
                mm.then_inc(h2t_done, 1)

            def layer3(t):
                pe.wait_ge(acc3_read, t + 1)
                pe.matmul(acc3[:, 0:H3], ones[2 * STACK:P, :], bias_w[2 * STACK:P, 0:H3],
                          start=True, stop=False)
                chunks = [(c, slice(c * H3, (c + 1) * H3)) for c in range(H2 // P)]
                i = W1_ITEMS + W2_ITEMS
                pe.wait_ge(h2hi_done, t + 1)
                for c, w in chunks:
                    pe.matmul(acc3[:, 0:H3], h2t_hi[:, c, :], w_hi[:, i, w], start=False, stop=False)
                    pe.matmul(acc3[:, 0:H3], h2t_hi[:, c, :], w_lo[:, i, w], start=False, stop=False)
                pe.wait_ge(h2lo_done, t + 1)
                for c, w in chunks:
                    mm = pe.matmul(acc3[:, 0:H3], h2t_lo[:, c, :], w_hi[:, i, w], start=False,
                                   stop=(c == H2 // P - 1))
                mm.then_inc(l3_done, 1)

            pe.wait_ge(ident_made, 1)
            pe.wait_ge(ones_made, 1)
            numeric_terms()

            def group(t, j, first):
                layer1(t, 2 * j, first)
                if j < GROUPS - 1:
                    turn_rows(t, j + 1, first)
                    layer1(t, 2 * j + 1, first)

            turn_rows(0, 0, True)
            start_layer1(0, True)
            for j in range(GROUPS):
                group(0, j, True)

            def tile(t, second):
                if not second:
                    layer3(t - 2)
                start_layer1(t, False)
                turn_hidden1(t - 1, second)
                turn_rows(t, 0, False)
                if second:
                    group(t, 0, False)
                    layer2(t - 1, 0, True)
                    group(t, 1, False)
                    layer2(t - 1, 1, True)
                else:
                    layer2(t - 1, 0, False)
                    group(t, 0, False)
                    layer2(t - 1, 1, False)
                    group(t, 1, False)
                group(t, 2, False)
                turn_hidden2(t - 1)
                for j in range(3, GROUPS):
                    group(t, j, False)

            tile(1, True)
            pe.wait_ge(hi_made, ITEMS)
            pe.wait_ge(lo_made, ITEMS)
            with pe.Fori(2, TILES) as t:
                tile(t, False)
            layer3(TILES - 2)
            turn_hidden1(TILES - 1, False)
            layer2(TILES - 1, 0, False)
            layer2(TILES - 1, 1, False)
            turn_hidden2(TILES - 1)
            layer3(TILES - 1)


def kernel(r_x_num, r_x_cat, L0_rec_bias, L0_rec_w_num, L0_rec_lin_cat, L0_rec_v_num, L0_rec_v_cat,
           L0_rec_W1, L0_rec_b1, L0_rec_W2, L0_rec_b2, L0_rec_W3, L0_rec_b3, L0_rec_Wo, L0_rec_bo):
    import numpy as np
    import concourse.bacc as bacc
    from concourse.bass_utils import run_bass_kernel_spmd

    f32 = np.float32
    x_num, x_cat = np.asarray(r_x_num), np.ascontiguousarray(r_x_cat)
    W1, W2, W3 = np.asarray(L0_rec_W1), np.asarray(L0_rec_W2), np.asarray(L0_rec_W3)
    v_cat, lin_cat = np.asarray(L0_rec_v_cat), np.asarray(L0_rec_lin_cat)
    table = np.empty((FIELDS, VOCAB, ROW), f32)
    table[0::2, :, 1:], table[0::2, :, :1] = v_cat[0::2], lin_cat[0::2]
    table[1::2, :, :K], table[1::2, :, K:] = v_cat[1::2], lin_cat[1::2]
    table = table.reshape(FIELDS * VOCAB, ROW)
    x_rows = np.zeros((STACK, BATCH + H2), f32)
    x_rows[:NUM, :BATCH] = x_num.T
    x_rows[NUM, :BATCH] = 1.0
    x_rows[0, BATCH:] = np.asarray(L0_rec_b2)
    num_weights = np.zeros((STACK, H1), f32)
    num_weights[:NUM] = W1[:NUM]
    num_weights[NUM] = np.asarray(L0_rec_b1)
    num_vectors = np.zeros((STACK, NV + H3), f32)
    num_vectors[:NUM, :K] = np.asarray(L0_rec_v_num)
    num_vectors[:NUM, K:K + 1] = np.asarray(L0_rec_w_num)
    num_vectors[0, NV:] = np.asarray(L0_rec_b3)
    row_consts = np.empty((P, H3 + 2), f32)
    row_consts[:, :H3] = np.asarray(L0_rec_Wo)[:, 0]
    row_consts[:, H3] = np.asarray(L0_rec_bias)
    row_consts[:, H3 + 1] = np.asarray(L0_rec_bo)
    weights = np.concatenate([
        W1[NUM:].reshape(W1_ITEMS, P, H1),
        W2.reshape(W2_ITEMS, 2, P, H2).transpose(0, 2, 1, 3).reshape(W2_ITEMS, P, H1),
        W3.reshape(W3_ITEMS, 4, P, H3).transpose(0, 2, 1, 3).reshape(W3_ITEMS, P, H1)])
    arrays = {"x_cat": x_cat, "table": table, "x_rows": x_rows, "num_weights": num_weights,
              "num_vectors": num_vectors, "row_consts": row_consts, "weights": weights}
    nc = bacc.Bacc("TRN2", target_bir_lowering=False, num_devices=1)
    args = [nc.dram_tensor(f"in_{name}", a.shape, mybir.dt.from_np(a.dtype), kind="ExternalInput").ap()
            for name, a in arrays.items()]
    out = nc.dram_tensor("out", (BATCH, 1), F32, kind="ExternalOutput").ap()
    deepfm_kernel(nc, *args, out)
    r = run_bass_kernel_spmd(nc, [{f"in_{name}": a for name, a in arrays.items()}], core_ids=[0])
    return r.results[0]["out"]
```

```python
from contextlib import ExitStack

import concourse.bass as bass
from concourse import mybir

P = 128
F32 = mybir.dt.float32
F32R = mybir.dt.float32r
BF16 = mybir.dt.bfloat16
I32 = mybir.dt.int32
ALU = mybir.AluOpType
ACT = mybir.ActivationFunctionType
AX = mybir.AxisListType

NUM = 13
FIELDS, VOCAB, K = 26, 12500, 64
ROW = K + 1
BATCH = 512
TILES = BATCH // P
H1, H2, H3 = 1024, 512, 256
CHUNKS = FIELDS * K // P
GROUPS = (CHUNKS + 1) // 2
HALF = 512
STACK = 32
NV = K + 2

W1_ITEMS, W2_ITEMS, W3_ITEMS = CHUNKS, (H1 // P) * H2 // H1, (H2 // P) * H3 // H1
W_ITEMS = W1_ITEMS + W2_ITEMS + W3_ITEMS
ITEMS = 2 + W_ITEMS
RING = 4


def fields_of(j):
    return 4 * j, min(4 * j + 4, FIELDS)


def chunks_of(j):
    return 2 * j, min(2 * j + 2, CHUNKS)


def x_slot(j):
    return 2 if j == GROUPS - 1 else j % 2


def items_in_group(j):
    return range(2 + chunks_of(j)[0], 2 + chunks_of(j)[1])


LATER_ITEMS = range(2 + W1_ITEMS, ITEMS)


def deepfm_kernel(nc, x_cat, table, x_rows, num_weights, num_vectors, row_consts, weights, out):
    with ExitStack() as ctx:
        def sb(name, shape, dt=F32):
            return ctx.enter_context(nc.sbuf_tensor(name, shape, dt))

        def ps(name, shape):
            return ctx.enter_context(nc.psum_tensor(name, shape, F32))

        def sem(name):
            return ctx.enter_context(nc.semaphore(name))

        cat = sb("cat", [P, TILES, FIELDS], I32)
        wrap = sb("wrap", [P, TILES * FIELDS])
        field_base = sb("field_base", [P, TILES, FIELDS], I32)
        row_all = sb("row_all", [P, TILES + 1, FIELDS], I32)
        row_now = sb("row_now", [P, FIELDS], I32)
        g = sb("g", [P, CHUNKS, 2 * ROW])
        ident = sb("ident", [P, P])
        ones = sb("ones", [P, P], F32R)
        raw = sb("raw", [P, RING, H1])
        w_hi = sb("w_hi", [P, W_ITEMS, H1], F32R)
        w_lo = sb("w_lo", [P, W_ITEMS, H1], F32R)
        num_w = sb("num_w", [P, H1], F32R)
        num_v = sb("num_v", [P, NV], F32R)
        bias_w = sb("bias_w", [P, HALF], F32R)
        consts = sb("consts", [P, H3 + 2])
        x_num_all = sb("x_num_all", [P, BATCH], F32R)
        x_num_now = sb("x_num_now", [P, P], F32R)
        v_sq = sb("v_sq", [STACK, 1])
        x_hi = sb("x_hi", [P, 5, P], F32R)
        x_lo = sb("x_lo", [P, 5, P], F32R)
        h1t_hi = sb("h1t_hi", [P, H1 // P, P], F32R)
        h1t_lo = sb("h1t_lo", [P, H1 // P, P], F32R)
        h2t_hi = sb("h2t_hi", [P, H2 // P, P], F32R)
        h2t_lo = sb("h2t_lo", [P, H2 // P, P], F32R)
        junk_sq = sb("junk_sq", [P, 4 * K], BF16)
        junk_h3 = sb("junk_h3", [P, H3], BF16)
        junk_fm = sb("junk_fm", [P, K], BF16)
        field_sum = sb("field_sum", [P, GROUPS, ROW])
        sq_sum = sb("sq_sum", [P, GROUPS])
        num_terms = sb("num_terms", [P, TILES, NV + 2])
        lin_const = sb("lin_const", [P, 1])
        num_sq_half = sb("num_sq_half", [P, TILES])
        s_vec = sb("s_vec", [P, ROW])
        s_all = sb("s_all", [P, ROW])
        fm_a = sb("fm_a", [P, 1])
        fm_b = sb("fm_b", [P, 1])
        fm_c = sb("fm_c", [P, 1])
        fm = sb("fm", [P, TILES])
        deep = sb("deep", [P, 1])
        result = sb("result", [P, TILES])
        h1 = sb("h1", [P, H1])
        h2 = sb("h2", [P, H2])
        x_sq = h1[0:STACK, 0:BATCH]
        vec_raw = h1[0:STACK, BATCH:BATCH + NV + H3]

        acc1 = [ps(f"acc1_{i}", [P, HALF]) for i in range(2)]
        xt_ps = [ps(f"xt_ps{i}", [P, HALF]) for i in range(2)]
        ht_ps = [ps(f"ht_ps{i}", [P, HALF]) for i in range(2)]
        acc2 = ps("acc2", [P, HALF])
        acc3 = ps("acc3", [P, HALF])

        cat_in = sem("cat_in")
        small_in = sem("small_in")
        raw_in = [sem(f"raw_in{s}") for s in range(RING)]
        rows_in = [sem(f"rows_in{j}") for j in range(GROUPS)]
        base_made = sem("base_made")
        zeros_made = sem("zeros_made")
        ones_made = sem("ones_made")
        ident_made = sem("ident_made")
        index_step = sem("index_step")
        rows_ready = sem("rows_ready")
        hi_made = sem("hi_made")
        lo_made = sem("lo_made")
        squares_made = sem("squares_made")
        num_lo_made = sem("num_lo_made")
        num_ps = sem("num_ps")
        num_step = sem("num_step")
        x_num_ready = sem("x_num_ready")
        num_added = sem("num_added")
        xt_done = sem("xt_done")
        xhi_done = sem("xhi_done")
        xlo_done = sem("xlo_done")
        l1_done = sem("l1_done")
        l1_half0 = sem("l1_half0")
        squared = sem("squared")
        summed = sem("summed")
        relu1a = sem("relu1a")
        relu1b = sem("relu1b")
        h1t_done = sem("h1t_done")
        h1hi_done = sem("h1hi_done")
        h1lo_done = sem("h1lo_done")
        l2_done = sem("l2_done")
        relu2 = sem("relu2")
        h2t_done = sem("h2t_done")
        h2hi_done = sem("h2hi_done")
        h2lo_done = sem("h2lo_done")
        l3_done = sem("l3_done")
        fm_step = sem("fm_step")
        fm_done = sem("fm_done")
        acc3_read = sem("acc3_read")
        result_done = sem("result_done")
        stored = sem("stored")

        block = ctx.enter_context(nc.Block())

        def x_cols(j):
            c0, c1 = chunks_of(j)
            s = 2 * x_slot(j)
            return slice(s, s + c1 - c0)

        def embeddings(j):
            c0, c1 = chunks_of(j)
            return g[:, c0:c1, 1:1 + 2 * K]

        def linear(j):
            c0, c1 = chunks_of(j)
            return g[:, c0:c1, 0:2 * ROW:2 * ROW - 1]

        @block.sync
        def _(sp):
            sp.dma_start(cat[:, :, :], x_cat.rearrange("(t p) f -> p t f", p=P)).then_inc(cat_in, 16)
            for i in range(ITEMS):
                if i >= RING:
                    sp.wait_ge(hi_made, i - RING + 1)
                    sp.wait_ge(lo_made, i - RING + 1)
                slot = raw[:, i % RING, :]
                if i == 0:
                    sp.dma_start(slot[0:STACK, :], num_weights).then_inc(raw_in[0], 16)
                elif i == 1:
                    sp.dma_start(slot[0:STACK, :], x_rows).then_inc(raw_in[1], 16)
                else:
                    sp.dma_start(slot, weights[i - 2]).then_inc(raw_in[i % RING], 16)
            with sp.Fori(0, TILES) as t:
                sp.wait_ge(result_done, t + 1)
                sp.dma_start(out[bass.ds(t * P, P), :], result[:, bass.ds(t, 1)]).then_inc(stored, 16)
            sp.wait_ge(stored, 16 * TILES)

        @block.gpsimd
        def _(pool):
            pool.iota(field_base[:, :, :], [[0, TILES], [VOCAB, FIELDS]], base=0,
                      channel_multiplier=0).then_inc(base_made, 1)
            pool.memset(row_all[:, TILES, :], 0).then_inc(base_made, 1)
            pool.memset(ident[:, :], 0.0).then_inc(zeros_made, 1)
            pool.wait_ge(zeros_made, 1)
            pool.affine_select(out=ident[:, :], in_=ident[:, :], compare_op=ALU.not_equal, fill=1.0,
                               base=0, pattern=[[-1, P]], channel_multiplier=1).then_inc(ident_made, 1)

            for t in range(TILES):
                for j in range(GROUPS):
                    pool.wait_ge(rows_ready, t * GROUPS + j + 1)
                    if t > 0:
                        pool.wait_ge(xt_done, (t - 1) * GROUPS + j + 1)
                        pool.wait_ge(squared, (t - 1) * GROUPS + j + 1)
                        pool.wait_ge(summed, 2 * ((t - 1) * GROUPS + j + 1))
                    for f in range(*fields_of(j)):
                        pool.indirect_dma_start(
                            g[:, f // 2, (f % 2) * ROW:(f % 2 + 1) * ROW], None, table,
                            bass.IndirectOffsetOnAxis(row_now[:, f:f + 1], 0)).then_inc(rows_in[j], 16)

        def rows_landed(eng, t, j):
            f0, f1 = fields_of(j)
            eng.wait_ge(rows_in[j], (t + 1) * 16 * (f1 - f0))

        def item_landed(eng, i):
            eng.wait_ge(raw_in[i % RING], 16 * (i // RING + 1))

        @block.scalar
        def _(act):
            act.dma_start(vec_raw, num_vectors).then_inc(small_in, 16)
            act.dma_start(consts[:, :], row_consts).then_inc(small_in, 16)

            def high_part(i):
                item_landed(act, i)
                act.activation(w_hi[:, i - 2, :], raw[:, i % RING, :], ACT.Copy).then_inc(hi_made, 1)

            def num_now(t):
                act.activation(x_num_now[:, :], x_num_all[:, bass.ds(t * P, P)].bitcast(F32),
                               ACT.Copy).then_inc(x_num_ready, 1)

            def high_stacks(tile, source, *stacks):
                for k in stacks:
                    last = act.activation(tile[k * STACK:(k + 1) * STACK, 0:source.shape[1]], source,
                                          ACT.Copy)
                return last

            item_landed(act, 0)
            high_stacks(num_w, raw[0:STACK, 0, :], 0, 2).then_inc(hi_made, 1)
            item_landed(act, 1)
            high_stacks(x_num_all, raw[0:STACK, 1, 0:BATCH], 0, 1).then_inc(hi_made, 1)
            act.activation(x_sq, raw[0:STACK, 1, 0:BATCH], ACT.Square).then_inc(squares_made, 1)
            high_stacks(bias_w, raw[0:STACK, 1, BATCH:BATCH + H2], 0).then_inc(squares_made, 1)
            act.wait_ge(small_in, 32)
            high_stacks(bias_w, vec_raw[:, NV:NV + H3], 2).then_inc(squares_made, 1)
            high_stacks(num_v, vec_raw[:, 0:NV], 0, 2).then_inc(squares_made, 1)
            act.activation(junk_sq[0:STACK, 0:K], vec_raw[:, 0:K], ACT.Square,
                           accum_out=v_sq[:, :]).then_inc(squares_made, 1)
            act.wait_ge(num_lo_made, 1)
            num_now(0)

            def group(t, j, first):
                n = t * GROUPS + j
                c0, c1 = chunks_of(j)
                width = (c1 - c0) * P
                if 2 <= j < GROUPS - 1:
                    act.wait_ge(l1_done, n - 1)
                elif not first:
                    act.wait_ge(l1_done, {0: n - 2, 1: n - 2, GROUPS - 1: n - GROUPS + 1}[j])
                act.wait_ge(xt_done, n + 1)
                act.activation(x_hi[:, x_cols(j), :], xt_ps[j % 2][:, 0:width], ACT.Copy)\
                   .then_inc(xhi_done, 1)
                f0, f1 = fields_of(j)
                rows_landed(act, t, j)
                if j == 0 and not first:
                    act.wait_ge(fm_done, t)
                if j == 0 and first:
                    act.wait_ge(squares_made, 5)
                else:
                    act.wait_ge(squared, n)
                act.activation(junk_sq[:, 0:(f1 - f0) * K], embeddings(j), ACT.Square,
                               accum_out=sq_sum[:, j:j + 1]).then_inc(squared, 1)

            def hidden1_high(t):
                for a in range(2):
                    act.wait_ge(h1t_done, 2 * t + a + 1)
                    act.activation(h1t_hi[:, 4 * a:4 * a + 4, :], ht_ps[a][:, :], ACT.Copy)\
                       .then_inc(h1hi_done, 1)

            def hidden2_relu(t):
                act.wait_ge(l2_done, t + 1)
                act.activation(h2[:, :], acc2[:, :], ACT.Relu).then_inc(relu2, 1)

            def hidden2_high(t):
                act.wait_ge(h2t_done, t + 1)
                act.activation(h2t_hi[:, :, :], ht_ps[0][:, :], ACT.Copy).then_inc(h2hi_done, 1)

            def hidden1_relu(t):
                act.wait_ge(l1_half0, t + 1)
                act.activation(h1[:, 0:HALF], acc1[0][:, :], ACT.Relu).then_inc(relu1a, 1)

            def tile_1():
                act.wait_ge(num_added, 1)
                num_now(1)
                hidden1_relu(0)
                group(1, 0, False)
                high_part(LATER_ITEMS[0])
                hidden1_high(0)
                group(1, 1, False)
                high_part(LATER_ITEMS[1])
                high_part(LATER_ITEMS[2])
                group(1, 2, False)
                high_part(LATER_ITEMS[3])
                high_part(LATER_ITEMS[4])
                group(1, 3, False)
                hidden2_relu(0)
                group(1, 4, False)
                hidden2_high(0)
                for j in range(5, GROUPS):
                    group(1, j, False)

            def tile(t):
                act.wait_ge(num_added, t)
                num_now(t)
                hidden1_relu(t - 1)
                hidden1_high(t - 1)
                group(t, 0, False)
                group(t, 1, False)
                group(t, 2, False)
                hidden2_relu(t - 1)
                group(t, 3, False)
                hidden2_high(t - 1)
                for j in range(4, GROUPS):
                    group(t, j, False)

            for j in range(GROUPS):
                for i in items_in_group(j):
                    high_part(i)
                group(0, j, True)
            tile_1()
            with act.Fori(2, TILES) as t:
                tile(t)
            hidden1_relu(TILES - 1)
            hidden1_high(TILES - 1)
            act.wait_ge(l2_done, TILES)
            act.activation(h2[:, 0:H2 // 2], acc2[:, 0:H2 // 2], ACT.Relu).then_inc(relu2, 1)
            act.activation(h2[:, H2 // 2:H2], acc2[:, H2 // 2:H2], ACT.Relu).then_inc(relu2, 1)
            for a in range(2):
                act.wait_ge(h2t_done, TILES + a)
                act.activation(h2t_hi[:, 2 * a:2 * a + 2, :], ht_ps[a][:, 0:2 * P], ACT.Copy)\
                   .then_inc(h2hi_done, 1)

        @block.vector
        def _(dve):
            flat = cat[:, :, :].rearrange("p t f -> p (t f)")
            rows = row_all[:, 0:TILES, :].rearrange("p t f -> p (t f)")
            base = field_base[:, :, :].rearrange("p t f -> p (t f)")
            dve.wait_ge(cat_in, 16)
            dve.tensor_scalar(wrap[:, :], flat, 0.0, float(VOCAB), ALU.is_lt, ALU.mult)\
               .then_inc(index_step, 1)
            dve.wait_ge(index_step, 1)
            dve.tensor_tensor(wrap[:, :], wrap[:, :], flat, ALU.add).then_inc(index_step, 1)
            dve.wait_ge(index_step, 2)
            dve.tensor_scalar(wrap[:, :], wrap[:, :], 0.0, float(VOCAB - 1), ALU.max, ALU.min)\
               .then_inc(index_step, 1)
            dve.wait_ge(index_step, 3)
            dve.wait_ge(base_made, 2)
            dve.tensor_tensor(row_now[:, :], wrap[:, 0:FIELDS], base[:, 0:FIELDS], ALU.add)\
               .then_inc(rows_ready, GROUPS)
            dve.tensor_tensor(rows, wrap[:, :], base, ALU.add).then_inc(index_step, 1)
            dve.memset(ones[:, :].bitcast(F32), 1.0).then_inc(ones_made, 1)

            def low_stacks(tile, source, high, *stacks):
                cols = slice(0, source.shape[1])
                for k in stacks:
                    last = dve.tensor_tensor(tile[k * STACK:(k + 1) * STACK, cols], source,
                                             tile[high * STACK:(high + 1) * STACK, cols].bitcast(F32),
                                             ALU.subtract)
                return last

            dve.wait_ge(hi_made, 1)
            low_stacks(num_w, raw[0:STACK, 0, :], 0, 1, 3).then_inc(lo_made, 1)
            dve.wait_ge(hi_made, 2)
            low_stacks(x_num_all, raw[0:STACK, 1, 0:BATCH], 0, 2, 3).then_inc(num_lo_made, 1)
            dve.wait_ge(squares_made, 5)
            low_stacks(bias_w, raw[0:STACK, 1, BATCH:BATCH + H2], 0, 1).then_inc(lo_made, 1)
            low_stacks(bias_w, vec_raw[:, NV:NV + H3], 2, 3).then_inc(num_lo_made, 1)
            low_stacks(num_v, vec_raw[:, 0:NV], 0, 1, 3).then_inc(num_lo_made, 1)

            def low_part(i):
                dve.wait_ge(hi_made, i + 1)
                dve.tensor_tensor(w_lo[:, i - 2, :], raw[:, i % RING, :],
                                  w_hi[:, i - 2, :].bitcast(F32), ALU.subtract).then_inc(lo_made, 1)

            def numeric_terms():
                dve.wait_ge(num_ps, 1)
                terms = acc3[:, 0:TILES * (NV + 2)].rearrange("p (t v) -> p t v", t=TILES)
                dve.tensor_copy(num_terms[:, :, 0:NV + 1], terms[:, :, 0:NV + 1])\
                   .then_inc(acc3_read, 1)
                dve.wait_ge(small_in, 32)
                dve.tensor_tensor(lin_const[:, :], consts[:, H3:H3 + 1], consts[:, H3 + 1:H3 + 2],
                                  ALU.add).then_inc(num_step, 1)
                dve.wait_ge(acc3_read, 1)
                dve.wait_ge(num_step, 1)
                dve.tensor_scalar(num_sq_half[:, :], num_terms[:, :, NV], -0.5, lin_const[:, :],
                                  ALU.mult, ALU.add).then_inc(num_step, 1)
                dve.wait_ge(num_step, 2)
                dve.tensor_tensor(num_terms[:, :, K], num_terms[:, :, K], num_sq_half[:, :],
                                  ALU.add).then_inc(num_step, 1)

            def group(t, j):
                n = t * GROUPS + j
                c0, c1 = chunks_of(j)
                width = (c1 - c0) * P
                f0, f1 = fields_of(j)
                dve.wait_ge(xhi_done, n + 1)
                dve.tensor_tensor(x_lo[:, x_cols(j), :],
                                  xt_ps[j % 2][:, 0:width].rearrange("p (c b) -> p c b", b=P),
                                  x_hi[:, x_cols(j), :].bitcast(F32), ALU.subtract).then_inc(xlo_done, 1)
                rows_landed(dve, t, j)
                dve.tensor_reduce(field_sum[:, j, 0:K],
                                  embeddings(j).rearrange("p c (a k) -> p k c a", a=2),
                                  AX.XY, ALU.add).then_inc(summed, 1)
                dve.tensor_reduce(field_sum[:, j, K:ROW], linear(j), AX.XY, ALU.add)\
                   .then_inc(summed, 1)
                dve.tensor_copy(row_now[:, f0:f1], row_all[:, t + 1, f0:f1]).then_inc(rows_ready, 1)

            def hidden1_low(t):
                for a in range(2):
                    dve.wait_ge(h1hi_done, 2 * t + a + 1)
                    dve.tensor_tensor(h1t_lo[:, 4 * a:4 * a + 4, :],
                                      ht_ps[a][:, :].rearrange("p (c b) -> p c b", b=P),
                                      h1t_hi[:, 4 * a:4 * a + 4, :].bitcast(F32), ALU.subtract)\
                       .then_inc(h1lo_done, 1)

            def hidden2_low(t):
                dve.wait_ge(h2hi_done, t + 1)
                dve.tensor_tensor(h2t_lo[:, :, :], ht_ps[0][:, :].rearrange("p (c b) -> p c b", b=P),
                                  h2t_hi[:, :, :].bitcast(F32), ALU.subtract).then_inc(h2lo_done, 1)

            def finish_tile(t):
                dve.wait_ge(l3_done, t + 1)
                dve.scalar_tensor_tensor(junk_h3[:, :], acc3[:, 0:H3], 0.0, consts[:, 0:H3],
                                         ALU.max, ALU.mult, accum_out=deep[:, :]).then_inc(acc3_read, 1)
                dve.wait_ge(acc3_read, t + 2)
                dve.wait_ge(fm_done, t + 1)
                dve.tensor_tensor(result[:, bass.ds(t, 1)], deep[:, :], fm[:, bass.ds(t, 1)], ALU.add).then_inc(result_done, 1)

            def hidden1_relu(t):
                dve.wait_ge(l1_done, (t + 1) * GROUPS)
                dve.tensor_scalar(h1[:, HALF:H1], acc1[1][:, :], 0.0, None, ALU.max).then_inc(relu1b, 1)

            def interactions(t):
                dve.wait_ge(summed, 2 * (t + 1) * GROUPS)
                dve.tensor_reduce(s_vec[:, :], field_sum[:, :, :].rearrange("p j k -> p k j"), AX.X,
                                  ALU.add).then_inc(fm_step, 1)
                dve.wait_ge(fm_step, 5 * t + 1)
                dve.tensor_tensor(s_all[:, :], s_vec[:, :], num_terms[:, t, 0:ROW], ALU.add)\
                   .then_inc(fm_step, 1)
                dve.wait_ge(squared, (t + 1) * GROUPS)
                dve.tensor_reduce(fm_b[:, :], sq_sum[:, :], AX.X, ALU.add).then_inc(fm_step, 1)
                dve.wait_ge(fm_step, 5 * t + 3)
                dve.tensor_tensor_reduce(junk_fm[:, :], s_all[:, 0:K], s_all[:, 0:K], 0.5, 0.0,
                                         ALU.mult, ALU.add, fm_a[:, :]).then_inc(fm_step, 1)
                dve.scalar_tensor_tensor(fm_c[:, :], fm_b[:, :], -0.5, s_all[:, K:ROW],
                                         ALU.mult, ALU.add).then_inc(fm_step, 1)
                dve.wait_ge(fm_step, 5 * t + 5)
                dve.tensor_tensor(fm[:, bass.ds(t, 1)], fm_c[:, :], fm_a[:, :], ALU.add).then_inc(fm_done, 1)

            def tile_1():
                hidden1_relu(0)
                group(1, 0)
                low_part(LATER_ITEMS[0])
                hidden1_low(0)
                group(1, 1)
                low_part(LATER_ITEMS[1])
                low_part(LATER_ITEMS[2])
                group(1, 2)
                low_part(LATER_ITEMS[3])
                low_part(LATER_ITEMS[4])
                group(1, 3)
                group(1, 4)
                hidden2_low(0)
                for j in range(5, GROUPS):
                    group(1, j)
                interactions(1)

            def tile(t):
                hidden1_relu(t - 1)
                finish_tile(t - 2)
                hidden1_low(t - 1)
                for j in range(4):
                    group(t, j)
                hidden2_low(t - 1)
                for j in range(4, GROUPS):
                    group(t, j)
                interactions(t)

            for j in range(GROUPS):
                for i in items_in_group(j):
                    low_part(i)
                group(0, j)
                if j == 0:
                    numeric_terms()
            dve.wait_ge(num_step, 3)
            interactions(0)
            tile_1()
            with dve.Fori(2, TILES) as t:
                tile(t)
            hidden1_relu(TILES - 1)
            finish_tile(TILES - 2)
            hidden1_low(TILES - 1)
            for a in range(2):
                dve.wait_ge(h2hi_done, TILES + a)
                dve.tensor_tensor(h2t_lo[:, 2 * a:2 * a + 2, :],
                                  ht_ps[a][:, 0:2 * P].rearrange("p (c b) -> p c b", b=P),
                                  h2t_hi[:, 2 * a:2 * a + 2, :].bitcast(F32), ALU.subtract)\
                   .then_inc(h2lo_done, 1)
            finish_tile(TILES - 1)

        @block.tensor
        def _(pe):
            def numeric_terms():
                pe.wait_ge(lo_made, 2)
                pe.wait_ge(num_lo_made, 3)
                for t in range(TILES):
                    at = t * (NV + 2)
                    pe.matmul(acc3[:, at:at + NV], x_num_all[:, t * P:(t + 1) * P], num_v[:, :],
                              start=True, stop=True)
                    mm = pe.matmul(acc3[:, at + NV:at + NV + 1], x_sq[:, t * P:(t + 1) * P], v_sq[:, :],
                                   start=True, stop=True)
                mm.then_inc(num_ps, 1)

            def turn_rows(t, j, first):
                n = t * GROUPS + j
                if j >= 2:
                    pe.wait_ge(xlo_done, n - 1)
                elif not first:
                    pe.wait_ge(xlo_done, {0: n, 1: n - 2}[j])
                rows_landed(pe, t, j)
                for a, c in enumerate(range(*chunks_of(j))):
                    mm = pe.transpose(xt_ps[j % 2][:, a * P:(a + 1) * P], g[:, c, 1:1 + P],
                                      ident[:, :])
                mm.then_inc(xt_done, 1)

            def start_layer1(t, first):
                pe.wait_ge(x_num_ready, t + 1)
                if not first:
                    pe.wait_ge(relu1a, t)
                    pe.wait_ge(relu1b, t)
                for a in range(2):
                    mm = pe.matmul(acc1[a][:, :], x_num_now[:, :], num_w[:, a * HALF:(a + 1) * HALF],
                                   start=True, stop=False)
                mm.then_inc(num_added, 1)

            def layer1(t, c, first):
                j = c // 2
                n = t * GROUPS + j
                last = c == CHUNKS - 1
                at = 2 * x_slot(j) + c % 2
                halves = [(acc1[a][:, :], slice(a * HALF, (a + 1) * HALF)) for a in range(2)]
                if first:
                    pe.wait_ge(hi_made, 2 + c + 1)
                    pe.wait_ge(lo_made, 2 + c + 1)
                pe.wait_ge(xhi_done, n + 1)
                for acc, w in halves:
                    pe.matmul(acc, x_hi[:, at, :], w_hi[:, c, w], start=False, stop=False)
                    pe.matmul(acc, x_hi[:, at, :], w_lo[:, c, w], start=False, stop=False)
                pe.wait_ge(xlo_done, n + 1)
                for a, (acc, w) in enumerate(halves):
                    mm = pe.matmul(acc, x_lo[:, at, :], w_hi[:, c, w], start=False, stop=last)
                    if last and a == 0:
                        mm.then_inc(l1_half0, 1)
                if last or c % 2:
                    mm.then_inc(l1_done, 1)

            def turn_hidden1(t, first):
                for a, relu in enumerate((relu1a, relu1b)):
                    pe.wait_ge(relu, t + 1)
                    if a == 0:
                        if not first:
                            pe.wait_ge(h2lo_done, t)
                    elif not first:
                        pe.wait_ge(h1lo_done, 2 * t)
                    for c in range(4):
                        mm = pe.transpose(ht_ps[a][:, c * P:(c + 1) * P],
                                          h1[:, a * HALF + c * P:a * HALF + (c + 1) * P], ident[:, :])
                    mm.then_inc(h1t_done, 1)

            def layer2(t, half, first):
                if half == 0:
                    if not first:
                        pe.wait_ge(relu2, t)
                    pe.matmul(acc2[:, :], ones[0:2 * STACK, :], bias_w[0:2 * STACK, :],
                              start=True, stop=False)
                chunks = [(c, W1_ITEMS + c // 2, slice(c % 2 * H2, (c % 2 + 1) * H2))
                          for c in range(4 * half, 4 * half + 4)]
                if first:
                    split = 2 + W1_ITEMS + 2 * half + 2
                    pe.wait_ge(hi_made, split)
                    pe.wait_ge(lo_made, split)
                pe.wait_ge(h1hi_done, 2 * t + half + 1)
                for c, i, w in chunks:
                    pe.matmul(acc2[:, :], h1t_hi[:, c, :], w_hi[:, i, w], start=False, stop=False)
                    pe.matmul(acc2[:, :], h1t_hi[:, c, :], w_lo[:, i, w], start=False, stop=False)
                pe.wait_ge(h1lo_done, 2 * t + half + 1)
                for c, i, w in chunks:
                    mm = pe.matmul(acc2[:, :], h1t_lo[:, c, :], w_hi[:, i, w], start=False,
                                   stop=(c == H1 // P - 1))
                if half == 1:
                    mm.then_inc(l2_done, 1)

            def turn_hidden2(t):
                pe.wait_ge(relu2, t + 1)
                pe.wait_ge(h1lo_done, 2 * t + 1)
                for c in range(4):
                    mm = pe.transpose(ht_ps[0][:, c * P:(c + 1) * P], h2[:, c * P:(c + 1) * P],
                                      ident[:, :])
                mm.then_inc(h2t_done, 1)

            def layer3(t):
                pe.wait_ge(acc3_read, t + 1)
                pe.matmul(acc3[:, 0:H3], ones[2 * STACK:P, :], bias_w[2 * STACK:P, 0:H3],
                          start=True, stop=False)
                chunks = [(c, slice(c * H3, (c + 1) * H3)) for c in range(H2 // P)]
                i = W1_ITEMS + W2_ITEMS
                pe.wait_ge(h2hi_done, t + 1)
                for c, w in chunks:
                    pe.matmul(acc3[:, 0:H3], h2t_hi[:, c, :], w_hi[:, i, w], start=False, stop=False)
                    pe.matmul(acc3[:, 0:H3], h2t_hi[:, c, :], w_lo[:, i, w], start=False, stop=False)
                pe.wait_ge(h2lo_done, t + 1)
                for c, w in chunks:
                    mm = pe.matmul(acc3[:, 0:H3], h2t_lo[:, c, :], w_hi[:, i, w], start=False,
                                   stop=(c == H2 // P - 1))
                mm.then_inc(l3_done, 1)

            def last_layer3():
                halves = [(a, range(2 * a, 2 * a + 2)) for a in range(2)]
                pe.wait_ge(acc3_read, TILES)
                pe.matmul(acc3[:, 0:H3], ones[2 * STACK:P, :], bias_w[2 * STACK:P, 0:H3],
                          start=True, stop=False)
                pe.wait_ge(h1lo_done, 2 * TILES)
                for a, chunks in halves:
                    pe.wait_ge(relu2, TILES + a)
                    for c in chunks:
                        mm = pe.transpose(ht_ps[a][:, c % 2 * P:(c % 2 + 1) * P],
                                          h2[:, c * P:(c + 1) * P], ident[:, :])
                    mm.then_inc(h2t_done, 1)
                i = W1_ITEMS + W2_ITEMS
                for a, chunks in halves:
                    pe.wait_ge(h2hi_done, TILES + a)
                    for c in chunks:
                        w = slice(c * H3, (c + 1) * H3)
                        pe.matmul(acc3[:, 0:H3], h2t_hi[:, c, :], w_hi[:, i, w], start=False, stop=False)
                        pe.matmul(acc3[:, 0:H3], h2t_hi[:, c, :], w_lo[:, i, w], start=False, stop=False)
                for a, chunks in halves:
                    pe.wait_ge(h2lo_done, TILES + a)
                    for c in chunks:
                        mm = pe.matmul(acc3[:, 0:H3], h2t_lo[:, c, :], w_hi[:, i, c * H3:(c + 1) * H3],
                                       start=False, stop=(c == H2 // P - 1))
                mm.then_inc(l3_done, 1)

            pe.wait_ge(ident_made, 1)
            pe.wait_ge(ones_made, 1)
            numeric_terms()

            def group(t, j, first):
                layer1(t, 2 * j, first)
                if j < GROUPS - 1:
                    turn_rows(t, j + 1, first)
                    layer1(t, 2 * j + 1, first)

            turn_rows(0, 0, True)
            start_layer1(0, True)
            for j in range(GROUPS):
                group(0, j, True)

            def tile_1():
                turn_rows(1, 0, False)
                start_layer1(1, False)
                turn_hidden1(0, True)
                group(1, 0, False)
                layer1(1, 2, False)
                layer2(0, 0, True)
                turn_rows(1, 2, False)
                layer1(1, 3, False)
                group(1, 2, False)
                layer2(0, 1, True)
                group(1, 3, False)
                turn_hidden2(0)
                for j in range(4, GROUPS):
                    group(1, j, False)

            def tile(t):
                layer3(t - 2)
                start_layer1(t, False)
                turn_hidden1(t - 1, False)
                turn_rows(t, 0, False)
                layer2(t - 1, 0, False)
                group(t, 0, False)
                layer2(t - 1, 1, False)
                group(t, 1, False)
                group(t, 2, False)
                turn_hidden2(t - 1)
                for j in range(3, GROUPS):
                    group(t, j, False)

            tile_1()
            pe.wait_ge(hi_made, ITEMS)
            pe.wait_ge(lo_made, ITEMS)
            with pe.Fori(2, TILES) as t:
                tile(t)
            layer3(TILES - 2)
            turn_hidden1(TILES - 1, False)
            layer2(TILES - 1, 0, False)
            layer2(TILES - 1, 1, False)
            last_layer3()


def kernel(r_x_num, r_x_cat, L0_rec_bias, L0_rec_w_num, L0_rec_lin_cat, L0_rec_v_num, L0_rec_v_cat,
           L0_rec_W1, L0_rec_b1, L0_rec_W2, L0_rec_b2, L0_rec_W3, L0_rec_b3, L0_rec_Wo, L0_rec_bo):
    import numpy as np
    import concourse.bacc as bacc
    from concourse.bass_utils import run_bass_kernel_spmd

    f32 = np.float32
    x_num, x_cat = np.asarray(r_x_num), np.ascontiguousarray(r_x_cat)
    W1, W2, W3 = np.asarray(L0_rec_W1), np.asarray(L0_rec_W2), np.asarray(L0_rec_W3)
    v_cat, lin_cat = np.asarray(L0_rec_v_cat), np.asarray(L0_rec_lin_cat)
    table = np.empty((FIELDS, VOCAB, ROW), f32)
    table[0::2, :, 1:], table[0::2, :, :1] = v_cat[0::2], lin_cat[0::2]
    table[1::2, :, :K], table[1::2, :, K:] = v_cat[1::2], lin_cat[1::2]
    table = table.reshape(FIELDS * VOCAB, ROW)
    x_rows = np.zeros((STACK, BATCH + H2), f32)
    x_rows[:NUM, :BATCH] = x_num.T
    x_rows[NUM, :BATCH] = 1.0
    x_rows[0, BATCH:] = np.asarray(L0_rec_b2)
    num_weights = np.zeros((STACK, H1), f32)
    num_weights[:NUM] = W1[:NUM]
    num_weights[NUM] = np.asarray(L0_rec_b1)
    num_vectors = np.zeros((STACK, NV + H3), f32)
    num_vectors[:NUM, :K] = np.asarray(L0_rec_v_num)
    num_vectors[:NUM, K:K + 1] = np.asarray(L0_rec_w_num)
    num_vectors[0, NV:] = np.asarray(L0_rec_b3)
    row_consts = np.empty((P, H3 + 2), f32)
    row_consts[:, :H3] = np.asarray(L0_rec_Wo)[:, 0]
    row_consts[:, H3] = np.asarray(L0_rec_bias)
    row_consts[:, H3 + 1] = np.asarray(L0_rec_bo)
    weights = np.concatenate([
        W1[NUM:].reshape(W1_ITEMS, P, H1),
        W2.reshape(W2_ITEMS, 2, P, H2).transpose(0, 2, 1, 3).reshape(W2_ITEMS, P, H1),
        W3.reshape(W3_ITEMS, 4, P, H3).transpose(0, 2, 1, 3).reshape(W3_ITEMS, P, H1)])
    arrays = {"x_cat": x_cat, "table": table, "x_rows": x_rows, "num_weights": num_weights,
              "num_vectors": num_vectors, "row_consts": row_consts, "weights": weights}
    nc = bacc.Bacc("TRN2", target_bir_lowering=False, num_devices=1)
    args = [nc.dram_tensor(f"in_{name}", a.shape, mybir.dt.from_np(a.dtype), kind="ExternalInput").ap()
            for name, a in arrays.items()]
    out = nc.dram_tensor("out", (BATCH, 1), F32, kind="ExternalOutput").ap()
    deepfm_kernel(nc, *args, out)
    r = run_bass_kernel_spmd(nc, [{f"in_{name}": a for name, a in arrays.items()}], core_ids=[0])
    return r.results[0]["out"]
```
